# Optimizing a Trainium2 kernel written in Bass

```python
import numpy as np
import jax
import jax.numpy as jnp

def _softmax(x, axis=-1):
    return jax.nn.softmax(x, axis=axis)

def _gelu(x):
    return jax.nn.gelu(x, approximate=True)

def _silu(x):
    return jax.nn.silu(x)

def _sigmoid(x):
    return jax.nn.sigmoid(x)

def _layernorm(x, axis=-1, eps=1e-05):
    m = jnp.mean(x, axis=axis, keepdims=True)
    v = jnp.var(x, axis=axis, keepdims=True)
    return (x - m) / jnp.sqrt(v + eps)

def _scatter_add(tgt, idx, src, axis=0):
    return tgt.at[idx].add(src)

def _segment_sum(src, seg, n):
    return jax.ops.segment_sum(src, seg, n)
kernel_name = 'mk_adj_preln_d2_adj_r2_b6dfd7'

def setup_inputs(seed: int=0):
    np.random.seed(seed)
    _w = jnp.asarray

    def _rec_inputs():
        import jax
        import jax.numpy as jnp
        _gk = jax.random.key(seed)
        x = 7.22e-05 + 1 * jax.random.normal(jax.random.fold_in(_gk, 1), (32, 256, 128), jnp.float32)
        _a = jax.random.bernoulli(jax.random.fold_in(_gk, 2), 0.015625, (32, 256, 256))
        _af = _a.astype(jnp.float32)
        adj = _af
        _nm = jnp.ones((32, 256), dtype=bool)
        nodemask = jnp.where(_nm, 1.0, 0.0).astype(jnp.float32)
        return (x, adj, nodemask)
    x, adj, nodemask = _rec_inputs()

    def _L0_gnn_setup():
        import jax, jax.numpy as jnp
        import numpy as np
        B, N, D, C, L = (64, 256, 128, 128, 5)
        EDGE_P = 0.02

        def _gru_cell(m, h, w_ih, w_hh, b_ih, b_hh):
            gi = m @ w_ih.T + b_ih
            gh = h @ w_hh.T + b_hh
            i_r, i_z, i_n = jnp.split(gi, 3, axis=-1)
            h_r, h_z, h_n = jnp.split(gh, 3, axis=-1)
            r = jax.nn.sigmoid(i_r + h_r)
            z = jax.nn.sigmoid(i_z + h_z)
            n = jnp.tanh(i_n + r * h_n)
            return (1.0 - z) * n + z * h
        key = jax.random.key(seed)
        ks = jax.random.split(key, 8)
        x = jax.random.normal(ks[0], (B, N, D), dtype=jnp.float32)
        adj = (jax.random.uniform(ks[1], (B, N, N)) < EDGE_P).astype(jnp.float32)
        mask = jnp.ones((B, N), dtype=jnp.float32)
        s = 1.0 / np.sqrt(C).astype(np.float32)
        weight = jax.random.uniform(ks[2], (L, C, C), minval=-s, maxval=s, dtype=jnp.float32)
        w_ih = jax.random.uniform(ks[3], (3 * C, C), minval=-s, maxval=s, dtype=jnp.float32)
        w_hh = jax.random.uniform(ks[4], (3 * C, C), minval=-s, maxval=s, dtype=jnp.float32)
        b_ih = jax.random.uniform(ks[5], (3 * C,), minval=-s, maxval=s, dtype=jnp.float32)
        b_hh = jax.random.uniform(ks[6], (3 * C,), minval=-s, maxval=s, dtype=jnp.float32)
        return dict(x=x, adj=adj, mask=mask, weight=weight, w_ih=w_ih, w_hh=w_hh, b_ih=b_ih, b_hh=b_hh)
    _L0_gnn_all = _L0_gnn_setup()
    _L0_gnn_in = {k: v for k, v in _L0_gnn_all.items() if k in ('weight', 'w_ih', 'w_hh', 'b_ih', 'b_hh')}
    del _L0_gnn_all

    def _L1_gnn_setup():
        import jax, jax.numpy as jnp
        import numpy as np
        B, N, C_IN, C_OUT = (8, 1024, 128, 128)
        key = jax.random.key(seed)
        k1, k2, k3 = jax.random.split(key, 3)
        x = jax.random.normal(k1, (B, N, C_IN), dtype=jnp.float32)
        adj = jax.random.uniform(k2, (B, N, N), dtype=jnp.float32)
        limit = float(np.sqrt(6.0 / (C_IN + C_OUT)))
        weight = jax.random.uniform(k3, (C_IN, C_OUT), minval=-limit, maxval=limit, dtype=jnp.float32)
        bias = jnp.zeros((C_OUT,), dtype=jnp.float32)
        return {'x': x, 'adj': adj, 'weight': weight, 'bias': bias}
    _L1_gnn_all = _L1_gnn_setup()
    _L1_gnn_in = {k: v for k, v in _L1_gnn_all.items() if k in ('weight', 'bias')}
    del _L1_gnn_all
    return {'x': x, 'adj': adj, 'nodemask': nodemask, 'L0_gnn_weight': _L0_gnn_in['weight'], 'L0_gnn_w_ih': _L0_gnn_in['w_ih'], 'L0_gnn_w_hh': _L0_gnn_in['w_hh'], 'L0_gnn_b_ih': _L0_gnn_in['b_ih'], 'L0_gnn_b_hh': _L0_gnn_in['b_hh'], 'L1_gnn_weight': _L1_gnn_in['weight'], 'L1_gnn_bias': _L1_gnn_in['bias']}

def reference(x, adj, nodemask, L0_gnn_weight, L0_gnn_w_ih, L0_gnn_w_hh, L0_gnn_b_ih, L0_gnn_b_hh, L1_gnn_weight, L1_gnn_bias):
    import jax
    import jax.numpy as jnp

    def _L0_gnn_ref(x, adj, mask, weight, w_ih, w_hh, b_ih, b_hh):
        import jax, jax.numpy as jnp
        import numpy as np
        B, N, D, C, L = (64, 256, 128, 128, 5)
        EDGE_P = 0.02

        def _gru_cell(m, h, w_ih, w_hh, b_ih, b_hh):
            gi = m @ w_ih.T + b_ih
            gh = h @ w_hh.T + b_hh
            i_r, i_z, i_n = jnp.split(gi, 3, axis=-1)
            h_r, h_z, h_n = jnp.split(gh, 3, axis=-1)
            r = jax.nn.sigmoid(i_r + h_r)
            z = jax.nn.sigmoid(i_z + h_z)
            n = jnp.tanh(i_n + r * h_n)
            return (1.0 - z) * n + z * h
        A = (adj != 0).astype(x.dtype)
        h = x
        for l in range(weight.shape[0]):
            m = jnp.einsum('bnd,de->bne', h, weight[l])
            agg = jnp.einsum('bij,bid->bjd', A, m)
            h = _gru_cell(agg, h, w_ih, w_hh, b_ih, b_hh)
        return h * mask[..., None]

    def _L1_gnn_ref(x, adj, weight, bias):
        import jax, jax.numpy as jnp
        import numpy as np
        B, N, C_IN, C_OUT = (8, 1024, 128, 128)
        d_inv_sqrt = (jnp.sum(adj, axis=-1) + 1e-05) ** (-0.5)
        adj_norm = d_inv_sqrt[..., :, None] * adj * d_inv_sqrt[..., None, :]
        support = jnp.einsum('bni,io->bno', x, weight)
        return jnp.einsum('bnm,bmo->bno', adj_norm, support) + bias
    h = jnp.maximum(_layernorm(x, axis=-1), 0.0)
    x = x + _L0_gnn_ref(h, adj, nodemask, L0_gnn_weight, L0_gnn_w_ih, L0_gnn_w_hh, L0_gnn_b_ih, L0_gnn_b_hh)
    h = jnp.maximum(_layernorm(x, axis=-1), 0.0)
    x = x + _L1_gnn_ref(h, adj, L1_gnn_weight, L1_gnn_bias)
    return x

_drawn_inputs = setup_inputs


def setup_inputs(seed=0):
    import zlib

    import numpy as np

    out = dict(_drawn_inputs(seed))
    spreads = {'L1_gnn_bias': (0.0, 2.0)}
    factors = {}
    for name, (base, spread) in spreads.items():
        noise = np.random.default_rng([zlib.crc32(name.encode()), seed]).standard_normal(out[name].shape)
        drawn = base * np.exp(spread * noise) if base else spread * noise
        out[name] = jnp.asarray(drawn.astype(out[name].dtype))
    for name, factor in factors.items():
        out[name] = (out[name] * factor).astype(out[name].dtype)
    return out
```

```python
import concourse.bass as bass
from concourse import mybir
from contextlib import ExitStack


def build(nc, x, adj, nodemask, w_msg, w_ih, w_hh, b_ih, b_hh, w_conv, b_conv, out):
    F32 = mybir.dt.float32
    F32R = mybir.dt.float32r
    ALU = mybir.AluOpType
    ACT = mybir.ActivationFunctionType
    AX = mybir.AxisListType

    B, N, D = x.shape
    L = w_msg.shape[0]
    P = 128
    K = N // P
    GB = 2
    T = GB * K
    COLS = T * P
    CH = 4
    ROUNDS = B // (GB * CH)
    STEPS = L * CH
    LAST = (L - 1) * CH
    ALL = STEPS * ROUNDS
    EPS = 1e-5
    NQ = 3

    x_v = x.rearrange("b n d -> (b n) d").rearrange("(g t p) d -> g p t d", t=T, p=P)
    out_v = out.rearrange("b n d -> (b n) d").rearrange("(g t p) d -> g p t d", t=T, p=P)
    adj_v = adj.rearrange("b n j -> (b n) j").rearrange("(g t p) j -> g p t j", t=T, p=P)

    ctx = ExitStack()
    with ctx:
        def sb(name, shape, dt=F32):
            return ctx.enter_context(nc.sbuf_tensor(name, shape, dt))

        def per_chain(name, shape, dt=F32, n=CH):
            return [sb(f"{name}{i}", shape, dt) for i in range(n)]

        def bank(name):
            return ctx.enter_context(nc.psum_tensor(name, [P, COLS], F32))

        def sem(name):
            return ctx.enter_context(nc.semaphore(name))

        ident = sb("ident", [P, P])
        minus_half = sb("minus_half", [P, 2 * T])
        eps = sb("eps", [P, 2 * T])
        w_conv_f = sb("w_conv_f", [P, P])
        n_mask_rows = B * K
        small_rows = sb("small_rows", [n_mask_rows + 2 * NQ, P])
        small_cols = sb("small_cols", [P, n_mask_rows + 2 * NQ])
        mask_cols = small_cols[:, 0:n_mask_rows]
        b_ih_cols = small_cols[:, n_mask_rows:n_mask_rows + NQ]
        b_hh_cols = small_cols[:, n_mask_rows + NQ:n_mask_rows + 2 * NQ]
        b_rz = sb("b_rz", [P, 2])
        b_out = sb("b_out", [P, T, P])
        u_hi = sb("u_hi", [P, L, NQ * P], F32R)
        u_lo = sb("u_lo", [P, L, NQ * P], F32R)
        v_hi = sb("v_hi", [P, NQ * P], F32R)
        v_lo = sb("v_lo", [P, NQ * P], F32R)
        c_hi = sb("c_hi", [P, P], F32R)
        c_lo = sb("c_lo", [P, P], F32R)

        h = per_chain("h", [P, COLS])
        h_hi = per_chain("h_hi", [P, COLS], F32R)
        h_lo = per_chain("h_lo", [P, COLS], F32R)
        h_end_all = sb("h_end_all", [P, CH * COLS])
        h_end = [h_end_all[:, c * COLS:(c + 1) * COLS] for c in range(CH)]
        n_hi = per_chain("n_hi", [P, T, P], F32R)
        n_lo = per_chain("n_lo", [P, T, P], F32R)
        edge = per_chain("edge", [P, T, N], F32R)
        h0 = per_chain("h0", [P, T, P])
        adj_a = per_chain("adj_a", [P, T, N], n=2)
        adj_b = per_chain("adj_b", [P, T, N])
        x2 = per_chain("x2", [P, T, P])
        h2_all = sb("h2_all", [P, 2 * COLS])
        h2 = [h2_all[:, i * COLS:(i + 1) * COLS].rearrange("p (t d) -> p t d", t=T) for i in range(2)]
        h2_hi = per_chain("h2_hi", [P, T, P], F32R)
        h2_lo = per_chain("h2_lo", [P, T, P], F32R)
        at_hi = per_chain("at_hi", [P, GB, K, N], F32R)
        at_lo = per_chain("at_lo", [P, GB, K, N], F32R)
        g_hi, g_lo = ([a[c][:, 0, :, :].rearrange("p k n -> p (k n)") for c in range(CH)] for a in (at_hi, at_lo))
        W3 = NQ * P
        w_ih_rows = h_end_all[:, 0:W3].rearrange("p (q e) -> p q e", q=NQ)
        w_hh_rows = h_end_all[:, W3:2 * W3].rearrange("p (q e) -> p q e", q=NQ)
        w_ih_t = h_end_all[:, 2 * W3:3 * W3]
        w_msg_rows = h_end_all[:, 3 * W3:3 * W3 + L * P].rearrange("p (l e) -> p l e", l=L)
        w_msg_t = h2_all[:, 0:L * P]
        p_hi = per_chain("p_hi", [P, COLS], F32R, n=2)
        p_lo = per_chain("p_lo", [P, COLS], F32R, n=2)
        r_g = per_chain("r_g", [P, COLS], n=2)
        z_g = per_chain("z_g", [P, COLS], n=2)
        cand = per_chain("cand", [P, COLS], n=2)
        zh = per_chain("zh", [P, COLS], n=2)
        st1 = per_chain("st1", [P, T, 6])
        st2 = per_chain("st2", [P, T, 6])
        mv1 = per_chain("mv1", [P, 2, T])
        mv2 = per_chain("mv2", [P, 3, T])
        spare = sb("spare", [P, 1])
        inv1 = per_chain("inv1", [P, T])
        inv2 = per_chain("inv2", [P, 2 * T])

        ps_hn = [bank("ps_hn0"), bank("ps_hn1")]
        ps_r, ps_z, ps_in, ps_p, ps_t, ps_x = (bank(n) for n in ("ps_r", "ps_z", "ps_in", "ps_p", "ps_t", "ps_x"))

        in_x1 = [sem(f"in_x1_{c}") for c in range(CH)]
        in_a1 = [sem(f"in_a1_{c}") for c in range(CH)]
        in_x2 = [sem(f"in_x2_{c}") for c in range(CH)]
        in_a2 = [sem(f"in_a2_{c}") for c in range(CH)]
        stored = [sem(f"stored_{c}") for c in range(CH)]
        in_w, in_msg, in_small, in_bias = sem("in_w"), sem("in_msg"), sem("in_small"), sem("in_bias")
        t_ready, p_ready, r_ready, z_ready, gates_ready = (
            sem(n) for n in ("t_ready", "p_ready", "r_ready", "z_ready", "gates_ready"))
        hend_t, adj_t, g_ready, y_ready = (sem(n) for n in ("hend_t", "adj_t", "g_ready", "y_ready"))
        t_hi, p_split_hi, r_done, z_done, n_done = (
            sem(n) for n in ("t_hi", "p_split_hi", "r_done", "z_done", "n_done"))
        h_hi_done = sem("h_hi_done")
        n_hi_first = sem("n_hi_first")
        h2_hi_done, at_hi_done, g_hi_done, y_done = (
            sem(n) for n in ("h2_hi_done", "at_hi_done", "g_hi_done", "y_done"))
        t_lo, p_split_lo, rhn_done, cand_done, zn_done, h_done = (
            sem(n) for n in ("t_lo", "p_split_lo", "rhn_done", "cand_done", "zn_done", "h_done"))
        st1_done, mv1_done, ln1_done, h0_done, edge_done = (
            sem(n) for n in ("st1_done", "mv1_done", "ln1_done", "h0_done", "edge_done"))
        adj_summed = sem("adj_summed")
        x2_done, st2_done, mv2_done, ln2_done, h2_done, at_lo_done, g_lo_done = (
            sem(n) for n in ("x2_done", "st2_done", "mv2_done", "ln2_done", "h2_done", "at_lo_done", "g_lo_done"))
        zh_done = sem("zh_done")
        h_lo_done = sem("h_lo_done")
        h_first, n_lo_first, ve1_done, inv1_done, ve2_done, inv2_done, x3_done, h2_lo_done, out_done = (
            sem(n) for n in ("h_first", "n_lo_first", "ve1_done", "inv1_done", "ve2_done", "inv2_done",
                             "x3_done", "h2_lo_done", "out_done"))
        ident0, ident_done, const_done = sem("ident0"), sem("ident_done"), sem("const_done")
        wt_ready, wt_act, wt_dve, u_ready, u_hi_done, u_lo_done = (
            sem(n) for n in ("wt_ready", "wt_act", "wt_dve", "u_ready", "u_hi_done", "u_lo_done"))

        SECOND = ([("h", c, 0) for c in range(CH)] + [("a", c, b) for c in range(CH) for b in range(GB)]
                  + [("g", 0, 0), ("g", 1, 0), ("y", 0, 0), ("g", 2, 0), ("y", 1, 0), ("g", 3, 0), ("y", 2, 0),
                     ("y", 3, 0)])
        assert len(SECOND) == STEPS

        SUM_ADJ, NORM2_STATS, NORM2, SPLIT_H2, ADD_BIAS = 0, 4, 7, 8, 11
        NORM1_STATS, NORM1, EDGES = 11, 14, 16

        class Round:

            def __init__(self, eng, r, first=None, last=None):
                self.eng, self.r = eng, r
                self.least, self.most = (r, r) if first is None else (first, last)
                self.base, self.counts, self.seen = {}, {}, {}

            def step(self, k):
                return 0 <= self.least * STEPS + k and self.most * STEPS + k < ALL

            def group(self, d):
                return 0 <= self.least + d and self.most + d < ROUNDS

            def value(self, per_round, count):
                if isinstance(self.r, int):
                    return self.r * per_round + count
                assert self.least * per_round + count >= 0
                if per_round not in self.base:
                    self.base[per_round] = self.eng.snap(self.r * per_round)
                key = per_round, count
                if key not in self.counts:
                    self.counts = {key: self.eng.snap(self.base[per_round] + count)}
                return self.counts[key]

            def wait(self, s, per_round, count):
                if self.most * per_round + count > 0 and count > self.seen.get(id(s), (s, count - 1))[1]:
                    self.seen[id(s)] = s, count
                    self.eng.wait_ge(s, self.value(per_round, count))

        def rounds(eng, body):
            body(Round(eng, -1))
            body(Round(eng, 0))
            with eng.Fori(1, ROUNDS - 1) as r:
                body(Round(eng, r, 1, ROUNDS - 2))
            body(Round(eng, ROUNDS - 1))
            body(Round(eng, ROUNDS))

        block = ctx.enter_context(nc.Block())

        @block.sync
        def _(sp):
            sp.dma_start(small_rows[0:n_mask_rows, :],
                         nodemask.rearrange("b (k p) -> (b k) p", p=P)).then_inc(in_small, 16)
            sp.dma_start(small_rows[n_mask_rows:n_mask_rows + NQ, :],
                         b_ih.rearrange("(q p) -> q p", p=P)).then_inc(in_small, 16)
            sp.dma_start(small_rows[n_mask_rows + NQ:n_mask_rows + 2 * NQ, :],
                         b_hh.rearrange("(q p) -> q p", p=P)).then_inc(in_small, 16)
            sp.dma_start(w_ih_rows, w_ih.rearrange("(q p) e -> p q e", p=P)).then_inc(in_w, 16)
            sp.dma_start(w_hh_rows, w_hh.rearrange("(q p) e -> p q e", p=P)).then_inc(in_w, 16)
            sp.dma_start(w_msg_rows, w_msg.rearrange("l d e -> d l e")).then_inc(in_msg, 16)

            def body(q):
                r = q.r
                if q.group(+1):
                    for c in range(CH):
                        q.wait(h_first, CH, c + 1)
                        sp.dma_start(h0[c][:], x_v[(r + 1) * CH + c]).then_inc(in_x1[c], 16)
                    for c in range(2):
                        q.wait(edge_done, CH, CH + c - 1)
                        sp.dma_start(adj_a[c][:], adj_v[(r + 1) * CH + c]).then_inc(in_a1[c], 16)
                if q.least == -1:
                    sp.dma_start(w_conv_f[:], w_conv).then_inc(in_bias, 16)
                    for t in range(T):
                        sp.dma_start(b_out[:, t, :],
                                     b_conv.rearrange("(o d) -> o d", o=1).broadcast_to((P, P))).then_inc(in_bias, 16)
                if q.group(0):
                    for c in range(CH):
                        q.wait(at_lo_done, GB * CH, -GB * CH + GB * (c + 1))
                        sp.dma_start(adj_b[c][:], adj_v[r * CH + c]).then_inc(in_a2[c], 16)
                if q.group(+1):
                    for c in range(2, CH):
                        q.wait(edge_done, CH, CH + c - 1)
                        sp.dma_start(adj_a[c - 2][:], adj_v[(r + 1) * CH + c]).then_inc(in_a1[c], 16)
                for c in range(CH + 1):
                    if q.group(-1) and c < CH:
                        q.wait(out_done, CH, -CH + c + 1)
                        sp.dma_start(out_v[(r - 1) * CH + c], x2[c][:]).then_inc(stored[c], 16)
                    if q.group(0) and c > 0:
                        q.wait(stored[c - 1], 16, 0)
                        sp.dma_start(x2[c - 1][:], x_v[r * CH + c - 1]).then_inc(in_x2[c - 1], 16)

            rounds(sp, body)
            for c in range(CH):
                sp.wait_ge(stored[c], 16 * ROUNDS)

        @block.tensor
        def _(pe):
            pe.wait_ge(ident_done, 1)
            pe.wait_ge(in_w, 32)
            for i in range(NQ):
                nc.tensor.transpose(ps_r[:, i * P:(i + 1) * P], w_ih_rows[:, i, :], ident[:])
            for i in range(NQ):
                last = nc.tensor.transpose(ps_z[:, i * P:(i + 1) * P], w_hh_rows[:, i, :], ident[:])
            last.then_inc(wt_ready, 1)
            pe.wait_ge(in_msg, 16)
            for l in range(L):
                ps = ps_in if l < 4 else ps_p
                last = nc.tensor.transpose(ps[:, l % 4 * P:(l % 4 + 1) * P], w_msg_rows[:, l, :], ident[:])
            last.then_inc(wt_ready, 1)
            pe.wait_ge(in_small, 48)
            n = n_mask_rows + 2 * NQ
            nc.tensor.transpose(ps_t[:, 0:n], small_rows[:], ident[0:n, 0:n]).then_inc(wt_ready, 1)
            pe.wait_ge(wt_act, 2)
            pe.wait_ge(wt_dve, 1)
            for l in range(L):
                if l >= 2:
                    pe.wait_ge(u_lo_done, l - 1)
                nc.tensor.matmul(ps_hn[l % 2][:, 0:NQ * P], w_msg_t[:, l * P:(l + 1) * P], w_ih_t,
                                 start=True, stop=True).then_inc(u_ready, 1)

            def mm3(o, w_hi, w_lo, m_hi, m_lo, start, stop):
                nc.tensor.matmul(o, w_hi, m_hi, start=start, stop=False)
                nc.tensor.matmul(o, w_hi, m_lo, start=False, stop=False)
                return nc.tensor.matmul(o, w_lo, m_hi, start=False, stop=stop)

            def gate_h(o, i, c, stop):
                w = slice(i * P, (i + 1) * P)
                return mm3(o[:], v_hi[:, w], v_lo[:, w], h_hi[c][:], h_lo[c][:], True, stop)

            def gate_m(o, i, l, k, start):
                w = slice(i * P, (i + 1) * P)
                return mm3(o[:], u_hi[:, l, w], u_lo[:, l, w], p_hi[k % 2][:], p_lo[k % 2][:], start, True)

            def hn_and_r(q, k):
                l, c = k // CH, k % CH
                if l:
                    q.wait(h_hi_done, LAST, k - CH + 1)
                    q.wait(h_lo_done, LAST, k - CH + 1)
                else:
                    q.wait(t_hi, STEPS, k + 1)
                    q.wait(t_lo, STEPS, k + 1)
                q.wait(rhn_done, STEPS, k - 1)
                gate_h(ps_hn[k % 2], 2, c, True)
                q.wait(r_done, STEPS, k)
                gate_h(ps_r, 0, c, False)
                q.wait(p_split_hi, STEPS, k + 1)
                q.wait(p_split_lo, STEPS, k + 1)
                gate_m(ps_r, 0, l, k, False).then_inc(r_ready, 1)

            def z_and_in(q, k):
                l, c = k // CH, k % CH
                q.wait(z_done, STEPS, k)
                gate_h(ps_z, 1, c, False)
                gate_m(ps_z, 1, l, k, False).then_inc(z_ready, 1)
                q.wait(cand_done, STEPS, k)
                gate_m(ps_in, 2, l, k, True).then_inc(gates_ready, 1)

            def aggregate(q, k):
                c = k % CH
                if k % STEPS < CH:
                    e = k // STEPS * CH + c + 1
                    q.wait(n_hi_first, CH, e)
                    q.wait(n_lo_first, CH, e)
                    q.wait(edge_done, CH, e)
                else:
                    q.wait(t_hi, STEPS, k + 1)
                    q.wait(t_lo, STEPS, k + 1)
                q.wait(p_split_hi, STEPS, k)
                q.wait(p_split_lo, STEPS, k)
                for b in range(GB):
                    for i in range(K):
                        t = b * K + i
                        o = ps_p[:, b * N:(b + 1) * N]
                        nc.tensor.matmul(o, n_hi[c][:, t, :], edge[c][:, t, :], start=(i == 0), stop=False)
                        last = nc.tensor.matmul(o, n_lo[c][:, t, :], edge[c][:, t, :],
                                                start=False, stop=(i == K - 1))
                last.then_inc(p_ready, 1)

            def transposes(q, k):
                c = k % CH
                if k % STEPS < CH:
                    q.wait(h0_done, CH, k // STEPS * CH + c + 1)
                else:
                    q.wait(h_done, STEPS, k - CH + 1)
                q.wait(t_hi, STEPS, k)
                q.wait(t_lo, STEPS, k)
                for t in range(T):
                    src = h0[c][:, t, :] if k % STEPS < CH else h[c][:, t * P:(t + 1) * P]
                    last = nc.tensor.transpose(ps_t[:, t * P:(t + 1) * P], src, ident[:])
                last.then_inc(t_ready, 1)

            def bank_x_read(q, k):
                kind, c, b = SECOND[k]
                if kind == "h":
                    q.wait(x2_done, CH, -CH + c + 1)
                elif kind == "a":
                    q.wait(at_hi_done, GB * CH, -GB * CH + GB * c + b + 1)
                    q.wait(at_lo_done, GB * CH, -GB * CH + GB * c + b + 1)
                elif kind == "g":
                    q.wait(g_hi_done, CH, -CH + c + 1)
                    q.wait(g_lo_done, CH, -CH + c + 1)
                else:
                    q.wait(y_done, CH, -CH + c + 1)

            def second_conv(q, k):
                kind, c, b = SECOND[k]
                if k:
                    bank_x_read(q, k - 1)
                else:
                    q.wait(y_done, CH, -CH)
                if kind == "h":
                    q.wait(h_done, STEPS, -CH + c + 1)
                    for t in range(T):
                        last = nc.tensor.transpose(ps_x[:, t * P:(t + 1) * P],
                                                   h_end[c][:, t * P:(t + 1) * P], ident[:])
                    last.then_inc(hend_t, 1)
                elif kind == "a":
                    q.wait(in_a2[c], 16, 0)
                    for i in range(K):
                        for n in range(K):
                            last = nc.tensor.transpose(
                                ps_x[:, i * N + n * P:i * N + (n + 1) * P],
                                adj_b[c][:, b * K + n, i * P:(i + 1) * P], ident[:])
                    last.then_inc(adj_t, 1)
                elif kind == "g":
                    q.wait(h2_hi_done, CH, -CH + c + 1)
                    q.wait(h2_lo_done, CH, -CH + c + 1)
                    for b in range(GB):
                        for i in range(K):
                            last = mm3(ps_x[:, b * N:(b + 1) * N],
                                       h2_hi[c][:, b * K + i, :], h2_lo[c][:, b * K + i, :],
                                       at_hi[c][:, b, i, :], at_lo[c][:, b, i, :], i == 0, i == K - 1)
                    last.then_inc(g_ready, 1)
                else:
                    q.wait(g_hi_done, CH, -CH + c + 1)
                    q.wait(g_lo_done, CH, -CH + c + 1)
                    for t in range(T):
                        w = slice(t * P, (t + 1) * P)
                        last = mm3(ps_x[:, w], g_hi[c][:, w], g_lo[c][:, w], c_hi[:], c_lo[:], True, True)
                    last.then_inc(y_ready, 1)

            pe.wait_ge(u_hi_done, L)
            pe.wait_ge(u_lo_done, L)
            pe.wait_ge(wt_act, 3)
            pe.wait_ge(wt_dve, 5)

            def body(q):
                for k in range(STEPS):
                    if q.step(k):
                        hn_and_r(q, k)
                    if q.step(k + 1):
                        aggregate(q, k + 1)
                    if q.step(k):
                        z_and_in(q, k)
                    if q.group(-1):
                        second_conv(q, k)
                    if q.step(k + 2):
                        transposes(q, k + 2)

            rounds(pe, body)

        @block.scalar
        def _(act):
            act.wait_ge(wt_ready, 1)
            nc.scalar.activation(v_hi[:], ps_z[:, 0:NQ * P], ACT.Copy).then_inc(wt_act, 1)
            act.wait_ge(wt_ready, 2)
            nc.scalar.activation(w_msg_t[:, 0:COLS], ps_in[:], ACT.Copy)
            nc.scalar.activation(w_msg_t[:, COLS:L * P], ps_p[:, 0:L * P - COLS], ACT.Copy).then_inc(wt_act, 1)
            for l in range(L):
                act.wait_ge(u_ready, l + 1)
                nc.scalar.activation(u_hi[:, l, :], ps_hn[l % 2][:, 0:NQ * P], ACT.Copy).then_inc(u_hi_done, 1)
            act.wait_ge(in_bias, 16 * (1 + T))
            nc.scalar.activation(c_hi[:], w_conv_f[:], ACT.Copy).then_inc(wt_act, 1)
            act.wait_ge(wt_dve, 4)

            def hi(dst, src):
                return nc.scalar.activation(dst, src, ACT.Copy)

            def leave_bank_x(q, k):
                kind, c, b = SECOND[k]
                if kind == "a":
                    q.wait(adj_t, GB * CH, -GB * CH + GB * c + b + 1)
                    hi(at_hi[c][:, b, :, :].rearrange("p k n -> p (k n)"), ps_x[:]).then_inc(at_hi_done, 1)
                elif kind == "g":
                    q.wait(g_ready, CH, -CH + c + 1)
                    hi(g_hi[c], ps_x[:]).then_inc(g_hi_done, 1)
                elif kind == "y":
                    q.wait(y_ready, CH, -CH + c + 1)
                    q.wait(h2_lo_done, CH, 0)
                    if c >= 2:
                        q.wait(out_done, CH, -CH + c - 1)
                    for t in range(T):
                        last = nc.scalar.activation(h2[c % 2][:, t, :], ps_x[:, t * P:(t + 1) * P], ACT.Copy,
                                                    scale=inv2[c][:, T + t:T + t + 1])
                    last.then_inc(y_done, 1)

            def body(q):
                for k in range(STEPS):
                    c_next = (k + 1) % CH
                    if q.step(k + 1):
                        q.wait(t_ready, STEPS, k + 2)
                        if (k + 1) % STEPS < CH:
                            q.wait(gates_ready, STEPS, k + 2 - CH)
                            hi(h_hi[c_next][:], ps_t[:]).then_inc(t_hi, 1)
                        else:
                            q.wait(p_ready, STEPS, k + 2 - CH)
                            hi(n_hi[c_next][:].rearrange("p t d -> p (t d)"), ps_t[:]).then_inc(t_hi, 1)
                    if q.step(k - 1):
                        q.wait(cand_done, STEPS, k)
                        nc.scalar.activation(cand[(k - 1) % 2][:], cand[(k - 1) % 2][:], ACT.Tanh,
                                             bias=b_ih_cols[:, 2:3]).then_inc(n_done, 1)
                    if q.step(k):
                        q.wait(r_ready, STEPS, k + 1)
                        q.wait(rhn_done, STEPS, k - 1)
                        nc.scalar.activation(r_g[k % 2][:], ps_r[:], ACT.Sigmoid,
                                             bias=b_rz[:, 0:1]).then_inc(r_done, 1)
                    if q.step(k - 1) and (k - 1) % STEPS < LAST:
                        q.wait(h_done, STEPS, k)
                        q.wait(gates_ready, STEPS, k)
                        hi(h_hi[(k - 1) % CH][:], h[(k - 1) % CH][:]).then_inc(h_hi_done, 1)
                    if q.step(k + 2) and (k + 2) % STEPS < CH:
                        c = (k + 2) % CH
                        q.wait(h0_done, CH, (k + 2) // STEPS * CH + c + 1)
                        q.wait(p_ready, STEPS, k + 3 - CH)
                        hi(n_hi[c][:], h0[c][:]).then_inc(n_hi_first, 1)
                    if q.step(k + 1):
                        q.wait(p_ready, STEPS, k + 2)
                        q.wait(gates_ready, STEPS, k)
                        hi(p_hi[(k + 1) % 2][:], ps_p[:]).then_inc(p_split_hi, 1)
                    if q.group(-1):
                        if 0 <= k - SPLIT_H2 < CH:
                            c = k - SPLIT_H2
                            q.wait(h2_done, CH, -CH + c + 1)
                            hi(h2_hi[c][:], h2[c % 2]).then_inc(h2_hi_done, 1)
                        if k:
                            leave_bank_x(q, k - 1)
                    if q.step(k):
                        q.wait(z_ready, STEPS, k + 1)
                        q.wait(zn_done, STEPS, k - 1)
                        q.wait(zh_done, STEPS, k - 1)
                        nc.scalar.activation(z_g[k % 2][:], ps_z[:], ACT.Sigmoid,
                                             bias=b_rz[:, 1:2]).then_inc(z_done, 1)
                if q.group(-1):
                    leave_bank_x(q, STEPS - 1)

            rounds(act, body)

        @block.vector
        def _(dve):
            dve.wait_ge(wt_ready, 1)
            nc.vector.tensor_copy(w_ih_t, ps_r[:, 0:NQ * P]).then_inc(wt_dve, 1)
            dve.wait_ge(wt_act, 1)
            nc.vector.tensor_tensor(v_lo[:], ps_z[:, 0:NQ * P], v_hi[:].bitcast(F32),
                                    ALU.subtract).then_inc(wt_dve, 1)
            dve.wait_ge(wt_ready, 3)
            nc.vector.tensor_copy(small_cols[:], ps_t[:, 0:n_mask_rows + 2 * NQ]).then_inc(wt_dve, 1)
            dve.wait_ge(wt_dve, 3)
            nc.vector.tensor_tensor(b_rz[:], b_ih_cols[:, 0:2], b_hh_cols[:, 0:2], ALU.add).then_inc(wt_dve, 1)
            for l in range(L):
                dve.wait_ge(u_hi_done, l + 1)
                nc.vector.tensor_tensor(u_lo[:, l, :], ps_hn[l % 2][:, 0:NQ * P], u_hi[:, l, :].bitcast(F32),
                                        ALU.subtract).then_inc(u_lo_done, 1)
            dve.wait_ge(wt_act, 3)
            nc.vector.tensor_tensor(c_lo[:], w_conv_f[:], c_hi[:].bitcast(F32), ALU.subtract).then_inc(wt_dve, 1)

            def lo(dst, src, part):
                return nc.vector.tensor_tensor(dst, src, part.bitcast(F32), ALU.subtract)

            def statistics(q, src, st, mv, st_done, mv_done, count):
                for t in range(T):
                    last = nc.vector.bn_stats(st[:, t, :], src[:, t, :])
                last.then_inc(st_done, 1)
                q.wait(st_done, CH, count)
                nc.vector.memset(spare[:], 0.0)
                for t in range(T):
                    last = nc.vector.bn_aggr(mv[:, 0:2, t], st[:, t, :])
                last.then_inc(mv_done, 1)

            def leave_bank_x(q, k):
                kind, c, b = SECOND[k]
                if kind == "h":
                    q.wait(hend_t, CH, -CH + c + 1)
                    q.wait(in_x2[c], 16, 0)
                    for t in range(T):
                        col = ((q.r - 1) * CH + c) * T + t
                        last = nc.vector.scalar_tensor_tensor(
                            x2[c][:, t, :], ps_x[:, t * P:(t + 1) * P], mask_cols[:, bass.ds(col, 1)],
                            x2[c][:, t, :], ALU.mult, ALU.add)
                    last.then_inc(x2_done, 1)
                elif kind == "a":
                    q.wait(at_hi_done, GB * CH, -GB * CH + GB * c + b + 1)
                    lo(at_lo[c][:, b, :, :].rearrange("p k n -> p (k n)"), ps_x[:],
                       at_hi[c][:, b, :, :].rearrange("p k n -> p (k n)")).then_inc(at_lo_done, 1)
                elif kind == "g":
                    q.wait(g_hi_done, CH, -CH + c + 1)
                    lo(g_lo[c], ps_x[:], g_hi[c]).then_inc(g_lo_done, 1)

            def before_work(q, k):
                if k:
                    leave_bank_x(q, k - 1)
                if 0 <= k - SUM_ADJ < CH:
                    c = k - SUM_ADJ
                    q.wait(in_a2[c], 16, 0)
                    nc.vector.reduce_sum(mv2[c][:, 2, :], adj_b[c][:], AX.X).then_inc(adj_summed, 1)
                if 0 <= k - NORM2_STATS < CH:
                    c = k - NORM2_STATS
                    q.wait(x2_done, CH, -CH + c + 1)
                    statistics(q, x2[c], st2[c], mv2[c], st2_done, mv2_done, -CH + c + 1)
                if 0 <= k - NORM2 < CH:
                    c = k - NORM2
                    q.wait(inv2_done, CH, -CH + c + 1)
                    if c < 2:
                        q.wait(out_done, CH, -CH)
                    else:
                        q.wait(h2_lo_done, CH, -CH + c - 1)
                    for t in range(T):
                        last = nc.vector.tensor_scalar(h2[c % 2][:, t, :], x2[c][:, t, :], mv2[c][:, 0, t:t + 1],
                                                       inv2[c][:, t:t + 1], ALU.subtract, ALU.mult)
                    last.then_inc(ln2_done, 1)
                    q.wait(ln2_done, CH, -CH + c + 1)
                    for t in range(T):
                        last = nc.vector.tensor_scalar(h2[c % 2][:, t, :], h2[c % 2][:, t, :], 0.0,
                                                       inv2[c][:, T + t:T + t + 1], ALU.max, ALU.mult)
                    last.then_inc(h2_done, 1)

            def after_work(q, k):
                if 0 <= k - NORM1_STATS < CH:
                    c = k - NORM1_STATS
                    q.wait(in_x1[c], 16, 32)
                    statistics(q, h0[c], st1[c], mv1[c], st1_done, mv1_done, CH + c + 1)
                if 0 <= k - NORM1 < CH:
                    c = k - NORM1
                    q.wait(inv1_done, CH, CH + c + 1)
                    for t in range(T):
                        last = nc.vector.tensor_scalar(h0[c][:, t, :], h0[c][:, t, :], mv1[c][:, 0, t:t + 1],
                                                       inv1[c][:, t:t + 1], ALU.subtract, ALU.mult)
                    last.then_inc(ln1_done, 1)
                    q.wait(ln1_done, CH, CH + c + 1)
                    nc.vector.tensor_scalar(h0[c][:], h0[c][:], 0.0, None, ALU.max).then_inc(h0_done, 1)
                if 0 <= k - EDGES < CH:
                    c = k - EDGES
                    q.wait(in_a1[c], 16, 32)
                    q.wait(p_ready, STEPS, LAST + c + 1)
                    nc.vector.tensor_scalar(edge[c][:], adj_a[c % 2][:], 0.0, None,
                                            ALU.not_equal).then_inc(edge_done, 1)

            def body(q):
                for k in range(STEPS):
                    c_next, c_last = (k + 1) % CH, (k - 1) % CH
                    if q.step(k + 1):
                        q.wait(t_hi, STEPS, k + 2)
                        if (k + 1) % STEPS < CH:
                            lo(h_lo[c_next][:], ps_t[:], h_hi[c_next][:]).then_inc(t_lo, 1)
                        else:
                            lo(n_lo[c_next][:].rearrange("p t d -> p (t d)"), ps_t[:],
                               n_hi[c_next][:].rearrange("p t d -> p (t d)")).then_inc(t_lo, 1)
                    if q.step(k - 1):
                        i = (k - 1) % 2
                        q.wait(n_done, STEPS, k)
                        nc.vector.scalar_tensor_tensor(cand[i][:], z_g[i][:], 1.0, cand[i][:],
                                                       ALU.subtract, ALU.mult).then_inc(zn_done, 1)
                        q.wait(zn_done, STEPS, k)
                        q.wait(zh_done, STEPS, k)
                        dst = h[c_last] if (k - 1) % STEPS < LAST else h_end[c_last]
                        nc.vector.tensor_tensor(dst[:], zh[i][:], cand[i][:], ALU.subtract).then_inc(h_done, 1)
                    if q.step(k):
                        q.wait(r_done, STEPS, k + 1)
                        nc.vector.scalar_tensor_tensor(cand[k % 2][:], ps_hn[k % 2][:], b_hh_cols[:, 2:3],
                                                       r_g[k % 2][:], ALU.add, ALU.mult).then_inc(rhn_done, 1)
                    if q.step(k + 1):
                        q.wait(p_split_hi, STEPS, k + 2)
                        lo(p_lo[(k + 1) % 2][:], ps_p[:], p_hi[(k + 1) % 2][:]).then_inc(p_split_lo, 1)
                    if q.group(-1):
                        before_work(q, k)
                    if q.group(+1):
                        after_work(q, k)
                    if q.step(k):
                        q.wait(gates_ready, STEPS, k + 1)
                        q.wait(rhn_done, STEPS, k + 1)
                        nc.vector.tensor_tensor(cand[k % 2][:], ps_in[:], cand[k % 2][:],
                                                ALU.add).then_inc(cand_done, 1)
                if q.group(-1):
                    leave_bank_x(q, STEPS - 1)

            rounds(dve, body)

        @block.gpsimd
        def _(pool):
            nc.gpsimd.memset(ident[:], 0.0).then_inc(ident0, 1)
            nc.gpsimd.memset(minus_half[:], -0.5).then_inc(const_done, 1)
            nc.gpsimd.memset(eps[:], EPS).then_inc(const_done, 1)
            pool.wait_ge(ident0, 1)
            nc.gpsimd.affine_select(out=ident[:], in_=ident[:], compare_op=ALU.not_equal, fill=1.0, base=0,
                                    pattern=[[-1, P]], channel_multiplier=1).then_inc(ident_done, 1)
            pool.wait_ge(const_done, 2)

            def inverse_roots(q, dst, src, added, done, count):
                nc.gpsimd.tensor_tensor(dst, src, eps[:, 0:dst.shape[1]], ALU.add).then_inc(added, 1)
                q.wait(added, CH, count)
                nc.gpsimd.tensor_tensor(dst, dst, minus_half[:, 0:dst.shape[1]], ALU.pow).then_inc(done, 1)

            def store_ready(q, k):
                kind, c, b = SECOND[k]
                if kind == "y":
                    q.wait(y_done, CH, -CH + c + 1)
                    q.wait(x3_done, CH, -CH + c + 1)
                    nc.gpsimd.tensor_tensor(x2[c][:], x2[c][:], h2[c % 2], ALU.add).then_inc(out_done, 1)

            def body(q):
                for k in range(STEPS):
                    c_next, c_last = (k + 1) % CH, (k - 1) % CH
                    if q.step(k + 1) and (k + 1) % STEPS < CH:
                        q.wait(t_lo, STEPS, k + 2)
                        nc.gpsimd.tensor_tensor(h[c_next][:], h_hi[c_next][:].bitcast(F32),
                                                h_lo[c_next][:].bitcast(F32), ALU.add).then_inc(h_first, 1)
                    if q.step(k - 1) and (k - 1) % STEPS < LAST:
                        q.wait(h_hi_done, LAST, k)
                        nc.gpsimd.tensor_tensor(h_lo[c_last][:], h[c_last][:], h_hi[c_last][:].bitcast(F32),
                                                ALU.subtract).then_inc(h_lo_done, 1)
                    if q.step(k + 2) and (k + 2) % STEPS < CH:
                        c = (k + 2) % CH
                        q.wait(n_hi_first, CH, (k + 2) // STEPS * CH + c + 1)
                        nc.gpsimd.tensor_tensor(n_lo[c][:], h0[c][:], n_hi[c][:].bitcast(F32),
                                                ALU.subtract).then_inc(n_lo_first, 1)
                    if q.group(-1):
                        if 0 <= k - NORM2_STATS < CH:
                            c = k - NORM2_STATS
                            q.wait(adj_summed, CH, -CH + c + 1)
                            q.wait(mv2_done, CH, -CH + c + 1)
                            inverse_roots(q, inv2[c][:], mv2[c][:, 1:3, :].rearrange("p s t -> p (s t)"),
                                          ve2_done, inv2_done, -CH + c + 1)
                        if 0 <= k - SPLIT_H2 < CH:
                            c = k - SPLIT_H2
                            q.wait(h2_hi_done, CH, -CH + c + 1)
                            nc.gpsimd.tensor_tensor(h2_lo[c][:], h2[c % 2], h2_hi[c][:].bitcast(F32),
                                                    ALU.subtract).then_inc(h2_lo_done, 1)
                        if 0 <= k - ADD_BIAS < CH:
                            c = k - ADD_BIAS
                            q.wait(ln2_done, CH, -CH + c + 1)
                            nc.gpsimd.tensor_tensor(x2[c][:], x2[c][:], b_out[:], ALU.add).then_inc(x3_done, 1)
                        if k:
                            store_ready(q, k - 1)
                    if q.group(+1) and 0 <= k - NORM1_STATS < CH:
                        c = k - NORM1_STATS
                        q.wait(mv1_done, CH, CH + c + 1)
                        inverse_roots(q, inv1[c][:], mv1[c][:, 1, :], ve1_done, inv1_done, CH + c + 1)
                    if q.step(k):
                        q.wait(z_done, STEPS, k + 1)
                        if k < CH:
                            q.wait(h_first, CH, k + 1)
                        nc.gpsimd.tensor_tensor(zh[k % 2][:], z_g[k % 2][:], h[k % CH][:],
                                                ALU.mult).then_inc(zh_done, 1)
                if q.group(-1):
                    store_ready(q, STEPS - 1)

            rounds(pool, body)


_INS = ["x", "adj", "nodemask", "L0_gnn_weight", "L0_gnn_w_ih", "L0_gnn_w_hh", "L0_gnn_b_ih", "L0_gnn_b_hh",
        "L1_gnn_weight", "L1_gnn_bias"]


def kernel(**inputs):
    import numpy as _np
    import concourse.bacc as _bacc
    from concourse import mybir as _mybir
    from concourse.bass_utils import run_bass_kernel_spmd as _run

    nc = _bacc.Bacc("TRN2", target_bir_lowering=False, num_devices=1)
    arrays, args = {}, []
    for name in _INS:
        a = _np.ascontiguousarray(inputs[name])
        arrays[f"in_{name}"] = a
        args.append(nc.dram_tensor(f"in_{name}", a.shape, _mybir.dt.from_np(a.dtype), kind="ExternalInput").ap())
    shape = inputs["x"].shape
    out = nc.dram_tensor("out", shape, _mybir.dt.from_np(_np.dtype("float32")), kind="ExternalOutput").ap()
    build(nc, *args, out)
    return _run(nc, [arrays], core_ids=[0]).results[0]["out"]
```

```python
import concourse.bass as bass
from concourse import mybir
from contextlib import ExitStack


def build(nc, x, adj, nodemask, w_msg, w_ih, w_hh, b_ih, b_hh, w_conv, b_conv, out):
    F32 = mybir.dt.float32
    F32R = mybir.dt.float32r
    ALU = mybir.AluOpType
    ACT = mybir.ActivationFunctionType
    AX = mybir.AxisListType

    B, N, D = x.shape
    L = w_msg.shape[0]
    P = 128
    K = N // P
    GB = 2
    T = GB * K
    COLS = T * P
    CH = 4
    ROUNDS = B // (GB * CH)
    STEPS = L * CH
    LAST = (L - 1) * CH
    ALL = STEPS * ROUNDS
    EPS = 1e-5
    NQ = 3

    x_v = x.rearrange("b n d -> (b n) d").rearrange("(g t p) d -> g p t d", t=T, p=P)
    out_v = out.rearrange("b n d -> (b n) d").rearrange("(g t p) d -> g p t d", t=T, p=P)
    adj_v = adj.rearrange("b n j -> (b n) j").rearrange("(g t p) j -> g p t j", t=T, p=P)

    ctx = ExitStack()
    with ctx:
        def sb(name, shape, dt=F32):
            return ctx.enter_context(nc.sbuf_tensor(name, shape, dt))

        def per_chain(name, shape, dt=F32, n=CH):
            return [sb(f"{name}{i}", shape, dt) for i in range(n)]

        def bank(name):
            return ctx.enter_context(nc.psum_tensor(name, [P, COLS], F32))

        def sem(name):
            return ctx.enter_context(nc.semaphore(name))

        ident = sb("ident", [P, P])
        minus_half = sb("minus_half", [P, 2 * T])
        eps = sb("eps", [P, 2 * T])
        zero = sb("zero", [P, T])
        w_conv_f = sb("w_conv_f", [P, P])
        n_mask_rows = B * K
        small_rows = sb("small_rows", [n_mask_rows + 2 * NQ, P])
        small_cols = sb("small_cols", [P, n_mask_rows + 2 * NQ])
        mask_cols = small_cols[:, 0:n_mask_rows]
        b_ih_cols = small_cols[:, n_mask_rows:n_mask_rows + NQ]
        b_hh_cols = small_cols[:, n_mask_rows + NQ:n_mask_rows + 2 * NQ]
        b_rz = sb("b_rz", [P, 2])
        b_out = sb("b_out", [P, T, P])
        u_hi = sb("u_hi", [P, L, NQ * P], F32R)
        u_lo = sb("u_lo", [P, L, NQ * P], F32R)
        v_hi = sb("v_hi", [P, NQ * P], F32R)
        v_lo = sb("v_lo", [P, NQ * P], F32R)
        c_hi = sb("c_hi", [P, P], F32R)
        c_lo = sb("c_lo", [P, P], F32R)

        h = per_chain("h", [P, COLS])
        h_hi = per_chain("h_hi", [P, COLS], F32R)
        h_lo = per_chain("h_lo", [P, COLS], F32R)
        h_end_all = sb("h_end_all", [P, CH * COLS])
        h_end = [h_end_all[:, c * COLS:(c + 1) * COLS] for c in range(CH)]
        n_hi = per_chain("n_hi", [P, T, P], F32R)
        n_lo = per_chain("n_lo", [P, T, P], F32R)
        edge = per_chain("edge", [P, T, N], F32R)
        h0 = per_chain("h0", [P, T, P])
        adj_a = per_chain("adj_a", [P, T, N], n=2)
        adj_b = per_chain("adj_b", [P, T, N])
        x2 = per_chain("x2", [P, T, P])
        h2_all = sb("h2_all", [P, 2 * COLS])
        h2 = [h2_all[:, i * COLS:(i + 1) * COLS].rearrange("p (t d) -> p t d", t=T) for i in range(2)]
        h2_hi = per_chain("h2_hi", [P, T, P], F32R)
        h2_lo = per_chain("h2_lo", [P, T, P], F32R)
        at_hi = per_chain("at_hi", [P, GB, K, N], F32R)
        at_lo = per_chain("at_lo", [P, GB, K, N], F32R)
        g_hi, g_lo = ([a[c][:, 0, :, :].rearrange("p k n -> p (k n)") for c in range(CH)] for a in (at_hi, at_lo))
        W3 = NQ * P
        w_ih_rows = h_end_all[:, 0:W3].rearrange("p (q e) -> p q e", q=NQ)
        w_hh_rows = h_end_all[:, W3:2 * W3].rearrange("p (q e) -> p q e", q=NQ)
        w_ih_t = h_end_all[:, 2 * W3:3 * W3]
        w_msg_rows = h_end_all[:, 3 * W3:3 * W3 + L * P].rearrange("p (l e) -> p l e", l=L)
        w_msg_t = h2_all[:, 0:L * P]
        p_hi = per_chain("p_hi", [P, COLS], F32R, n=2)
        p_lo = per_chain("p_lo", [P, COLS], F32R, n=2)
        r_g = per_chain("r_g", [P, COLS], n=2)
        z_g = per_chain("z_g", [P, COLS], n=2)
        cand = per_chain("cand", [P, COLS], n=2)
        zh = per_chain("zh", [P, COLS], n=2)
        st1 = per_chain("st1", [P, T, 6])
        st2 = per_chain("st2", [P, T, 6])
        mv1 = per_chain("mv1", [P, 2, T])
        mv2 = per_chain("mv2", [P, 3, T])
        spare, spare_act = sb("spare", [P, 1]), sb("spare_act", [P, 1])
        inv1 = per_chain("inv1", [P, T])
        inv2 = per_chain("inv2", [P, 2 * T])
        inv2d = per_chain("inv2d", [P, T])
        shift1 = per_chain("shift1", [P, T])
        shift2 = per_chain("shift2", [P, T])

        ps_hn = [bank("ps_hn0"), bank("ps_hn1")]
        ps_r, ps_z, ps_in, ps_p, ps_t, ps_x = (bank(n) for n in ("ps_r", "ps_z", "ps_in", "ps_p", "ps_t", "ps_x"))

        in_x1 = [sem(f"in_x1_{c}") for c in range(CH)]
        in_a1 = [sem(f"in_a1_{c}") for c in range(CH)]
        in_x2 = [sem(f"in_x2_{c}") for c in range(CH)]
        in_a2 = [sem(f"in_a2_{c}") for c in range(CH)]
        stored = [sem(f"stored_{c}") for c in range(CH)]
        in_w, in_msg, in_small, in_conv, in_bias = (
            sem(n) for n in ("in_w", "in_msg", "in_small", "in_conv", "in_bias"))
        t_ready, p_ready, r_ready, z_ready, gates_ready = (
            sem(n) for n in ("t_ready", "p_ready", "r_ready", "z_ready", "gates_ready"))
        hend_t, adj_t, g_ready, y_ready = (sem(n) for n in ("hend_t", "adj_t", "g_ready", "y_ready"))
        t_hi, p_split_hi, r_done, z_done, n_done = (
            sem(n) for n in ("t_hi", "p_split_hi", "r_done", "z_done", "n_done"))
        h_hi_done = sem("h_hi_done")
        n_hi_first = sem("n_hi_first")
        h0_done, ln2_done, adj_summed = sem("h0_done"), sem("ln2_done"), sem("adj_summed")
        h2_hi_done, at_hi_done, g_hi_done, y_done = (
            sem(n) for n in ("h2_hi_done", "at_hi_done", "g_hi_done", "y_done"))
        t_lo, p_split_lo, rhn_done, cand_done, zn_done, h_done = (
            sem(n) for n in ("t_lo", "p_split_lo", "rhn_done", "cand_done", "zn_done", "h_done"))
        st1_done, mv1_done, edge_done = (
            sem(n) for n in ("st1_done", "mv1_done", "edge_done"))
        x2_done, st2_done, mv2_done, at_lo_done, g_lo_done = (
            sem(n) for n in ("x2_done", "st2_done", "mv2_done", "at_lo_done", "g_lo_done"))
        zh_done = sem("zh_done")
        h_lo_done = sem("h_lo_done")
        h_first, n_lo_first, ve1_done, inv1_done, ve2_done, inv2_done, x3_done, h2_lo_done, out_done = (
            sem(n) for n in ("h_first", "n_lo_first", "ve1_done", "inv1_done", "ve2_done", "inv2_done",
                             "x3_done", "h2_lo_done", "out_done"))
        inv2d_done = sem("inv2d_done")
        mi1_done, shift1_done, mi2_done, shift2_done = (
            sem(n) for n in ("mi1_done", "shift1_done", "mi2_done", "shift2_done"))
        ident0, ident_done, const_done = sem("ident0"), sem("ident_done"), sem("const_done")
        wt_ready, wt_act, wt_dve, u_ready, u_hi_done, u_lo_done = (
            sem(n) for n in ("wt_ready", "wt_act", "wt_dve", "u_ready", "u_hi_done", "u_lo_done"))

        def slots(at, d):
            out = {}
            for c, k in enumerate(at):
                out.setdefault(k, []).append((c, d))
            return out

        def joined(*parts):
            out = {}
            for part in parts:
                for k, work in part.items():
                    out.setdefault(k, []).extend(work)
            return out

        CONV = {k: [(p[0], int(p[1]), int(p[2]), -1)] for k, p in enumerate(
            "h00 a00 h10 a01 h20 a10 h30 a11 a20 a21 a30 a31 g00 g10 y00 g20 y10 g30 y20 y30".split())}

        def products(text):
            out = {}
            for word in text.split():
                k, p = word.split(":")
                out.setdefault(int(k), []).append((p[0], int(p[1]), int(p[2]), 0 if p.endswith("'") else -1))
            return out

        CONV_LAST_MID = products("1:a00 2:a10 3:a11 4:a21 5:a30 9:g10 11:g20 13:g30 "
                                 "14:a00' 15:a01' 16:a11' 17:a21' 18:a31'")
        CONV_LAST = products("0:h00 1:a01 2:h10 3:a20 4:h20 5:a31 6:h30 7:g00 11:y00 12:y10 13:y20 14:y30 "
                             "15:a10' 16:a20' 17:a30' 18:h00' 19:h10'")
        CONV_END = products("0:h20 1:h30 2:g00 3:g10 4:y00 5:g20 6:y10 7:g30 8:y20 9:y30")

        STEADY = dict(
            conv=CONV, conv_mid={}, banks=[ps_x],
            sum_adj=slots([0, 1, 2, 4], -1), stats2=slots([2, 4, 6, 8], -1), norm2=slots([3, 5, 7, 9], -1),
            split2=slots([6, 8, 10, 12], -1), split2_lo=slots([6, 8, 10, 12], -1), bias=slots([5, 7, 9, 11], -1),
            stats1=slots([12, 14, 15, 17], 1), norm1=slots([13, 15, 16, 18], 1), edges=slots([16, 17, 18, 19], 1))
        START = dict(STEADY, stats1=slots([14, 16, 18, 19], 1), norm1=slots([17, 18, 19], 1),
                     edges=slots([17, 18], 1))
        FIRST = dict(STEADY, norm1=joined(STEADY["norm1"], {0: [(3, 0)]}),
                     edges=joined(STEADY["edges"], {0: [(2, 0)], 1: [(3, 0)]}))
        LAST_ROUND = dict(STEADY, conv=CONV_LAST, conv_mid=CONV_LAST_MID,
                          sum_adj=joined(STEADY["sum_adj"], slots([12, 13, 15, 16], 0)),
                          stats2=joined(STEADY["stats2"], {19: [(0, 0)]}))
        END = dict(STEADY, conv=CONV_END, banks=[ps_x, ps_r, ps_z, ps_in], sum_adj={},
                   stats2={0: [(1, -1)], 1: [(2, -1)], 2: [(3, -1)]}, norm2=slots([0, 1, 2, 3], -1),
                   split2=slots([0, 1, 2, 3], -1), split2_lo=slots([2, 3, 4, 5], -1), bias=slots([1, 2, 3, 4], -1))

        class Round:

            def __init__(self, eng, r, first=None, last=None):
                self.eng, self.r = eng, r
                self.least, self.most = (r, r) if first is None else (first, last)
                self.base, self.counts, self.seen = {}, {}, {}
                self.end = self.least == ROUNDS
                self.plan = {-1: START, 0: FIRST, ROUNDS - 1: LAST_ROUND, ROUNDS: END}.get(self.least, STEADY)
                self.products = [p for k in range(STEPS)
                                 for p in self.work("conv_mid", k) + self.work("conv", k)]

            def work(self, name, k):
                return [w for w in self.plan[name].get(k, []) if self.group(w[-1])]

            def bank(self, product):
                banks = self.plan["banks"]
                return banks[self.products.index(product) % len(banks)]

            def before(self, product):
                i = self.products.index(product) - len(self.plan["banks"])
                return self.products[i] if i >= 0 else None

            def step(self, k):
                return 0 <= self.least * STEPS + k and self.most * STEPS + k < ALL

            def group(self, d):
                return 0 <= self.least + d and self.most + d < ROUNDS

            def value(self, per_round, count):
                if isinstance(self.r, int):
                    return self.r * per_round + count
                assert self.least * per_round + count > 0, (per_round, count)
                if per_round not in self.base:
                    self.base[per_round] = self.eng.snap(self.r * per_round)
                key = per_round, count
                if key not in self.counts:
                    self.counts = {key: self.eng.snap(self.base[per_round] + count)}
                return self.counts[key]

            def wait(self, s, per_round, count):
                if self.most * per_round + count > 0 and count > self.seen.get(id(s), (s, count - 1))[1]:
                    self.seen[id(s)] = s, count
                    self.eng.wait_ge(s, self.value(per_round, count))

        UNITS = [15, 16, 17, 18, 18]

        def rounds(eng, body):
            body(Round(eng, -1))
            body(Round(eng, 0))
            with eng.Fori(1, ROUNDS - 1) as r:
                body(Round(eng, r, 1, ROUNDS - 2))
            body(Round(eng, ROUNDS - 1))
            body(Round(eng, ROUNDS))

        block = ctx.enter_context(nc.Block())

        @block.sync
        def _(sp):
            sp.dma_start(w_ih_rows, w_ih.rearrange("(q p) e -> p q e", p=P)).then_inc(in_w, 16)
            sp.dma_start(w_hh_rows, w_hh.rearrange("(q p) e -> p q e", p=P)).then_inc(in_w, 16)
            sp.dma_start(w_msg_rows, w_msg.rearrange("l d e -> d l e")).then_inc(in_msg, 16)

            def body(q):
                r = q.r
                if q.group(+1):
                    for c in range(CH):
                        q.wait(h_first, CH, c + 1)
                        sp.dma_start(h0[c][:], x_v[(r + 1) * CH + c]).then_inc(in_x1[c], 16)
                        if q.least == -1 and c == 0:
                            sp.dma_start(small_rows[0:n_mask_rows, :],
                                         nodemask.rearrange("b (k p) -> (b k) p", p=P)).then_inc(in_small, 16)
                            sp.dma_start(small_rows[n_mask_rows:n_mask_rows + NQ, :],
                                         b_ih.rearrange("(q p) -> q p", p=P)).then_inc(in_small, 16)
                            sp.dma_start(small_rows[n_mask_rows + NQ:n_mask_rows + 2 * NQ, :],
                                         b_hh.rearrange("(q p) -> q p", p=P)).then_inc(in_small, 16)
                        if q.least == -1 and c == 1:
                            sp.dma_start(w_conv_f[:], w_conv).then_inc(in_conv, 16)
                        if c < 2:
                            q.wait(edge_done, CH, CH + c - 1)
                            sp.dma_start(adj_a[c][:], adj_v[(r + 1) * CH + c]).then_inc(in_a1[c], 16)
                if q.least == -1:
                    for t in range(T):
                        sp.dma_start(b_out[:, t, :],
                                     b_conv.rearrange("(o d) -> o d", o=1).broadcast_to((P, P))).then_inc(in_bias, 16)
                if q.group(0):
                    for c in range(CH):
                        q.wait(at_lo_done, GB * CH, -GB * CH + GB * (c + 1))
                        sp.dma_start(adj_b[c][:], adj_v[r * CH + c]).then_inc(in_a2[c], 16)
                if q.group(+1):
                    for c in range(2, CH):
                        q.wait(edge_done, CH, CH + c - 1)
                        sp.dma_start(adj_a[c - 2][:], adj_v[(r + 1) * CH + c]).then_inc(in_a1[c], 16)
                for c in range(CH + 1):
                    if q.group(-1) and c < CH:
                        q.wait(out_done, CH, -CH + c + 1)
                        sp.dma_start(out_v[(r - 1) * CH + c], x2[c][:]).then_inc(stored[c], 16)
                    if q.group(0) and c > 0:
                        q.wait(stored[c - 1], 16, 0)
                        sp.dma_start(x2[c - 1][:], x_v[r * CH + c - 1]).then_inc(in_x2[c - 1], 16)

            rounds(sp, body)
            for c in range(CH):
                sp.wait_ge(stored[c], 16 * ROUNDS)

        @block.tensor
        def _(pe):
            pe.wait_ge(ident_done, 1)
            pe.wait_ge(in_w, 32)
            for i in range(NQ):
                nc.tensor.transpose(ps_r[:, i * P:(i + 1) * P], w_ih_rows[:, i, :], ident[:])
            for i in range(NQ):
                last = nc.tensor.transpose(ps_z[:, i * P:(i + 1) * P], w_hh_rows[:, i, :], ident[:])
            last.then_inc(wt_ready, 1)
            pe.wait_ge(in_msg, 16)
            for l in range(L):
                ps = ps_in if l < 4 else ps_p
                last = nc.tensor.transpose(ps[:, l % 4 * P:(l % 4 + 1) * P], w_msg_rows[:, l, :], ident[:])
            last.then_inc(wt_ready, 1)
            pe.wait_ge(wt_act, 2)
            pe.wait_ge(wt_dve, 1)
            for l in range(L):
                if l >= 2:
                    pe.wait_ge(u_lo_done, l - 1)
                nc.tensor.matmul(ps_hn[l % 2][:, 0:NQ * P], w_msg_t[:, l * P:(l + 1) * P], w_ih_t,
                                 start=True, stop=True).then_inc(u_ready, 1)
                if l == 1:
                    pe.wait_ge(in_small, 48)
                    n = n_mask_rows + 2 * NQ
                    nc.tensor.transpose(ps_t[:, 0:n], small_rows[:], ident[0:n, 0:n]).then_inc(wt_ready, 1)

            def mm3(o, w_hi, w_lo, m_hi, m_lo, start, stop):
                nc.tensor.matmul(o, w_hi, m_hi, start=start, stop=False)
                nc.tensor.matmul(o, w_hi, m_lo, start=False, stop=False)
                return nc.tensor.matmul(o, w_lo, m_hi, start=False, stop=stop)

            def gate_h(o, i, c, stop):
                w = slice(i * P, (i + 1) * P)
                return mm3(o[:], v_hi[:, w], v_lo[:, w], h_hi[c][:], h_lo[c][:], True, stop)

            def gate_m(o, i, l, k, start):
                w = slice(i * P, (i + 1) * P)
                return mm3(o[:], u_hi[:, l, w], u_lo[:, l, w], p_hi[k % 2][:], p_lo[k % 2][:], start, True)

            def hn_and_r(q, k):
                l, c = k // CH, k % CH
                if l:
                    q.wait(h_hi_done, LAST, k - CH + 1)
                    q.wait(h_lo_done, LAST, k - CH + 1)
                else:
                    q.wait(t_hi, STEPS, k + 1)
                    q.wait(t_lo, STEPS, k + 1)
                q.wait(rhn_done, STEPS, k - 1)
                gate_h(ps_hn[k % 2], 2, c, True)
                q.wait(r_done, STEPS, k)
                gate_h(ps_r, 0, c, False)
                q.wait(p_split_hi, STEPS, k + 1)
                q.wait(p_split_lo, STEPS, k + 1)
                gate_m(ps_r, 0, l, k, False).then_inc(r_ready, 1)

            def z_and_in(q, k):
                l, c = k // CH, k % CH
                q.wait(z_done, STEPS, k)
                gate_h(ps_z, 1, c, False)
                gate_m(ps_z, 1, l, k, False).then_inc(z_ready, 1)
                q.wait(cand_done, STEPS, k)
                gate_m(ps_in, 2, l, k, True).then_inc(gates_ready, 1)

            def aggregate(q, k):
                c = k % CH
                if k % STEPS < CH:
                    e = k // STEPS * CH + c + 1
                    q.wait(n_hi_first, CH, e)
                    q.wait(n_lo_first, CH, e)
                    q.wait(edge_done, CH, e)
                else:
                    q.wait(t_hi, STEPS, k + 1)
                    q.wait(t_lo, STEPS, k + 1)
                q.wait(p_split_hi, STEPS, k)
                q.wait(p_split_lo, STEPS, k)
                for b in range(GB):
                    for i in range(K):
                        t = b * K + i
                        o = ps_p[:, b * N:(b + 1) * N]
                        nc.tensor.matmul(o, n_hi[c][:, t, :], edge[c][:, t, :], start=(i == 0), stop=False)
                        last = nc.tensor.matmul(o, n_lo[c][:, t, :], edge[c][:, t, :],
                                                start=False, stop=(i == K - 1))
                last.then_inc(p_ready, 1)

            def transposes(q, k):
                c = k % CH
                if k % STEPS < CH:
                    q.wait(h0_done, CH, k // STEPS * CH + c + 1)
                else:
                    q.wait(h_done, STEPS, k - CH + 1)
                q.wait(t_hi, STEPS, k)
                q.wait(t_lo, STEPS, k)
                for t in range(T):
                    src = h0[c][:, t, :] if k % STEPS < CH else h[c][:, t * P:(t + 1) * P]
                    last = nc.tensor.transpose(ps_t[:, t * P:(t + 1) * P], src, ident[:])
                last.then_inc(t_ready, 1)

            def has_left(q, product):
                kind, c, b, d = product
                if kind == "h":
                    q.wait(x2_done, CH, CH * d + c + 1)
                elif kind == "a":
                    q.wait(at_hi_done, GB * CH, GB * (CH * d + c) + b + 1)
                    q.wait(at_lo_done, GB * CH, GB * (CH * d + c) + b + 1)
                elif kind == "g":
                    q.wait(g_hi_done, CH, CH * d + c + 1)
                    q.wait(g_lo_done, CH, CH * d + c + 1)
                else:
                    q.wait(out_done if q.end else y_done, CH, CH * d + c + 1)

            def second_conv(q, product):
                kind, c, b, d = product
                if q.before(product):
                    has_left(q, q.before(product))
                elif q.end:
                    q.wait(x2_done, CH, 2 - CH)
                    q.wait(z_done, STEPS, 0)
                    q.wait(cand_done, STEPS, 0)
                else:
                    q.wait(t_hi, STEPS, 2)
                ps = q.bank(product)
                if kind == "h":
                    q.wait(h_done, STEPS, STEPS * d + LAST + c + 1)
                    for t in range(T):
                        last = nc.tensor.transpose(ps[:, t * P:(t + 1) * P],
                                                   h_end[c][:, t * P:(t + 1) * P], ident[:])
                    last.then_inc(hend_t, 1)
                elif kind == "a":
                    q.wait(in_a2[c], 16, 16 * (d + 1))
                    for i in range(K):
                        for n in range(K):
                            last = nc.tensor.transpose(
                                ps[:, i * N + n * P:i * N + (n + 1) * P],
                                adj_b[c][:, b * K + n, i * P:(i + 1) * P], ident[:])
                    last.then_inc(adj_t, 1)
                elif kind == "g":
                    q.wait(h2_hi_done, CH, CH * d + c + 1)
                    q.wait(h2_lo_done, CH, CH * d + c + 1)
                    q.wait(at_hi_done, GB * CH, GB * (CH * d + c + 1))
                    q.wait(at_lo_done, GB * CH, GB * (CH * d + c + 1))
                    for b in range(GB):
                        for i in range(K):
                            last = mm3(ps[:, b * N:(b + 1) * N],
                                       h2_hi[c][:, b * K + i, :], h2_lo[c][:, b * K + i, :],
                                       at_hi[c][:, b, i, :], at_lo[c][:, b, i, :], i == 0, i == K - 1)
                    last.then_inc(g_ready, 1)
                else:
                    q.wait(g_hi_done, CH, CH * d + c + 1)
                    q.wait(g_lo_done, CH, CH * d + c + 1)
                    for t in range(T):
                        w = slice(t * P, (t + 1) * P)
                        last = mm3(ps[:, w], g_hi[c][:, w], g_lo[c][:, w], c_hi[:], c_lo[:], True, True)
                    last.then_inc(y_ready, 1)

            pe.wait_ge(wt_dve, 3)

            def body(q):
                if q.least == 0:
                    pe.wait_ge(u_hi_done, L)
                    pe.wait_ge(u_lo_done, L)
                for k in range(STEPS):
                    if q.step(k):
                        hn_and_r(q, k)
                    if q.step(k + 1):
                        aggregate(q, k + 1)
                    for product in q.work("conv_mid", k):
                        second_conv(q, product)
                    if q.step(k):
                        z_and_in(q, k)
                    for product in q.work("conv", k):
                        second_conv(q, product)
                    if q.step(k + 2):
                        transposes(q, k + 2)

                if q.least == 0:
                    pe.wait_ge(wt_act, 3)
                    pe.wait_ge(wt_dve, 5)

            rounds(pe, body)

        @block.scalar
        def _(act):
            act.wait_ge(const_done, 4)
            nc.scalar.activation(spare_act[:], spare_act[:], ACT.Sigmoid)
            act.wait_ge(wt_ready, 1)
            nc.scalar.activation(v_hi[:], ps_z[:, 0:NQ * P], ACT.Copy).then_inc(wt_act, 1)
            act.wait_ge(wt_ready, 2)
            nc.scalar.activation(w_msg_t[:, 0:COLS], ps_in[:], ACT.Copy)
            nc.scalar.activation(w_msg_t[:, COLS:L * P], ps_p[:, 0:L * P - COLS], ACT.Copy).then_inc(wt_act, 1)

            def weights(k):
                for l in range(L):
                    if UNITS[l] == k:
                        act.wait_ge(u_ready, l + 1)
                        nc.scalar.activation(u_hi[:, l, :], ps_hn[l % 2][:, 0:NQ * P],
                                             ACT.Copy).then_inc(u_hi_done, 1)
                if k == STEPS - 1:
                    act.wait_ge(in_conv, 16)
                    nc.scalar.activation(c_hi[:], w_conv_f[:], ACT.Copy).then_inc(wt_act, 1)
                    act.wait_ge(wt_dve, 4)

            def hi(dst, src):
                return nc.scalar.activation(dst, src, ACT.Copy)

            def leave(q, product):
                kind, c, b, d = product
                ps = q.bank(product)
                if kind == "a":
                    q.wait(adj_summed, CH, CH * d + c + 1)
                    q.wait(adj_t, GB * CH, GB * (CH * d + c) + b + 1)
                    hi(at_hi[c][:, b, :, :].rearrange("p k n -> p (k n)"), ps[:]).then_inc(at_hi_done, 1)
                elif kind == "g":
                    q.wait(g_ready, CH, CH * d + c + 1)
                    hi(g_hi[c], ps[:]).then_inc(g_hi_done, 1)
                elif kind == "y":
                    if not q.end:
                        q.wait(y_ready, CH, CH * d + c + 1)
                        q.wait(h2_lo_done, CH, CH * d + min(c + 3, CH))
                        if c >= 2:
                            q.wait(out_done, CH, CH * d + c - 1)
                        for t in range(T):
                            last = nc.scalar.activation(h2[c % 2][:, t, :], ps[:, t * P:(t + 1) * P], ACT.Copy,
                                                        scale=inv2[c][:, T + t:T + t + 1])
                        last.then_inc(y_done, 1)

            def sum_adj(q, c, d):
                q.wait(in_a2[c], 16, 16 * (d + 1))
                for t in range(T):
                    last = nc.scalar.activation(at_hi[c][:, t // K, t % K, :], adj_b[c][:, t, :],
                                                ACT.Copy, accum_out=mv2[c][:, 2, t:t + 1])
                last.then_inc(adj_summed, 1)

            def norm(dst, src, inv, shift):
                for t in range(T):
                    last = nc.scalar.activation(dst[:, t, :], src[:, t, :], ACT.Relu,
                                                bias=shift[:, t:t + 1], scale=inv[:, t:t + 1])
                return last

            def body(q):
                for k in range(STEPS):
                    c_next = (k + 1) % CH
                    if q.least < 0:
                        weights(k)
                    if q.step(k + 1):
                        q.wait(t_ready, STEPS, k + 2)
                        if (k + 1) % STEPS < CH:
                            q.wait(gates_ready, STEPS, k + 2 - CH)
                            hi(h_hi[c_next][:], ps_t[:]).then_inc(t_hi, 1)
                        else:
                            q.wait(p_ready, STEPS, k + 2 - CH)
                            hi(n_hi[c_next][:].rearrange("p t d -> p (t d)"), ps_t[:]).then_inc(t_hi, 1)
                    if q.step(k - 1):
                        q.wait(cand_done, STEPS, k)
                        nc.scalar.activation(cand[(k - 1) % 2][:], cand[(k - 1) % 2][:], ACT.Tanh,
                                             bias=b_ih_cols[:, 2:3]).then_inc(n_done, 1)
                    for product in q.work("conv", k - 1):
                        leave(q, product)
                    if q.step(k):
                        q.wait(r_ready, STEPS, k + 1)
                        q.wait(rhn_done, STEPS, k - 1)
                        nc.scalar.activation(r_g[k % 2][:], ps_r[:], ACT.Sigmoid,
                                             bias=b_rz[:, 0:1]).then_inc(r_done, 1)
                    if q.step(k + 1):
                        q.wait(p_ready, STEPS, k + 2)
                        q.wait(gates_ready, STEPS, k)
                        hi(p_hi[(k + 1) % 2][:], ps_p[:]).then_inc(p_split_hi, 1)
                    if q.step(k - 1) and (k - 1) % STEPS < LAST:
                        q.wait(h_done, STEPS, k)
                        q.wait(gates_ready, STEPS, k)
                        hi(h_hi[(k - 1) % CH][:], h[(k - 1) % CH][:]).then_inc(h_hi_done, 1)
                    for product in q.work("conv_mid", k):
                        leave(q, product)
                    if q.step(k + 2) and (k + 2) % STEPS < CH:
                        c = (k + 2) % CH
                        q.wait(h0_done, CH, (k + 2) // STEPS * CH + c + 1)
                        q.wait(p_ready, STEPS, k + 3 - CH)
                        hi(n_hi[c][:], h0[c][:]).then_inc(n_hi_first, 1)
                    for c, d in q.work("norm1", k):
                        q.wait(shift1_done, CH, CH * d + c + 1)
                        norm(h0[c], h0[c], inv1[c], shift1[c]).then_inc(h0_done, 1)
                    for c, d in q.work("norm2", k):
                        q.wait(shift2_done, CH, CH * d + c + 1)
                        q.wait(x2_done, CH, CH * d + c + 1)
                        if c >= 2:
                            q.wait(h2_lo_done, CH, CH * d + c - 1)
                        norm(h2[c % 2], x2[c], inv2d[c], shift2[c]).then_inc(ln2_done, 1)
                    for c, d in q.work("sum_adj", k):
                        sum_adj(q, c, d)
                    for c, d in q.work("split2", k):
                        q.wait(ln2_done, CH, CH * d + c + 1)
                        hi(h2_hi[c][:], h2[c % 2]).then_inc(h2_hi_done, 1)
                    if q.step(k):
                        q.wait(z_ready, STEPS, k + 1)
                        q.wait(zn_done, STEPS, k - 1)
                        q.wait(zh_done, STEPS, k - 1)
                        nc.scalar.activation(z_g[k % 2][:], ps_z[:], ACT.Sigmoid,
                                             bias=b_rz[:, 1:2]).then_inc(z_done, 1)
                for product in q.work("conv", STEPS - 1):
                    leave(q, product)

            rounds(act, body)

        @block.vector
        def _(dve):
            dve.wait_ge(wt_ready, 1)
            nc.vector.tensor_copy(w_ih_t, ps_r[:, 0:NQ * P]).then_inc(wt_dve, 1)
            dve.wait_ge(wt_act, 1)
            nc.vector.tensor_tensor(v_lo[:], ps_z[:, 0:NQ * P], v_hi[:].bitcast(F32),
                                    ALU.subtract).then_inc(wt_dve, 1)

            def weights(k):
                for l in range(L):
                    if UNITS[l] == k:
                        dve.wait_ge(u_hi_done, l + 1)
                        nc.vector.tensor_tensor(u_lo[:, l, :], ps_hn[l % 2][:, 0:NQ * P],
                                                u_hi[:, l, :].bitcast(F32), ALU.subtract).then_inc(u_lo_done, 1)
                if k == UNITS[1]:
                    dve.wait_ge(wt_ready, 3)
                    nc.vector.tensor_copy(small_cols[:], ps_t[:, 0:n_mask_rows + 2 * NQ]).then_inc(wt_dve, 1)
                    dve.wait_ge(wt_dve, 3)
                    nc.vector.tensor_tensor(b_rz[:], b_ih_cols[:, 0:2], b_hh_cols[:, 0:2],
                                            ALU.add).then_inc(wt_dve, 1)

            def last_weight():
                dve.wait_ge(wt_act, 3)
                nc.vector.tensor_tensor(c_lo[:], w_conv_f[:], c_hi[:].bitcast(F32), ALU.subtract).then_inc(wt_dve, 1)

            def lo(dst, src, part):
                return nc.vector.tensor_tensor(dst, src, part.bitcast(F32), ALU.subtract)

            def statistics(q, src, st, mv, st_done, mv_done, count):
                for t in range(T):
                    last = nc.vector.bn_stats(st[:, t, :], src[:, t, :])
                last.then_inc(st_done, 1)
                q.wait(st_done, CH, count)
                nc.vector.memset(spare[:], 0.0)
                for t in range(T):
                    last = nc.vector.bn_aggr(mv[:, 0:2, t], st[:, t, :])
                last.then_inc(mv_done, 1)

            def leave(q, product):
                kind, c, b, d = product
                ps = q.bank(product)
                if kind == "h":
                    q.wait(hend_t, CH, CH * d + c + 1)
                    q.wait(in_x2[c], 16, 16 * (d + 1))
                    for t in range(T):
                        col = ((q.r + d) * CH + c) * T + t
                        last = nc.vector.scalar_tensor_tensor(
                            x2[c][:, t, :], ps[:, t * P:(t + 1) * P], mask_cols[:, bass.ds(col, 1)],
                            x2[c][:, t, :], ALU.mult, ALU.add)
                    last.then_inc(x2_done, 1)
                elif kind == "a":
                    q.wait(at_hi_done, GB * CH, GB * (CH * d + c) + b + 1)
                    lo(at_lo[c][:, b, :, :].rearrange("p k n -> p (k n)"), ps[:],
                       at_hi[c][:, b, :, :].rearrange("p k n -> p (k n)")).then_inc(at_lo_done, 1)
                elif kind == "g":
                    q.wait(g_hi_done, CH, CH * d + c + 1)
                    lo(g_lo[c], ps[:], g_hi[c]).then_inc(g_lo_done, 1)
                elif q.end:
                    q.wait(y_ready, CH, CH * d + c + 1)
                    q.wait(x3_done, CH, CH * d + c + 1)
                    for t in range(T):
                        last = nc.vector.scalar_tensor_tensor(
                            x2[c][:, t, :], ps[:, t * P:(t + 1) * P], inv2[c][:, T + t:T + t + 1],
                            x2[c][:, t, :], ALU.mult, ALU.add)
                    last.then_inc(out_done, 1)

            def extras(q, k):
                for c, d in q.work("edges", k):
                    q.wait(in_a1[c], 16, 16 * (d + 1))
                    q.wait(p_ready, STEPS, STEPS * (d - 1) + LAST + c + 1)
                    nc.vector.tensor_scalar(edge[c][:], adj_a[c % 2][:], 0.0, None,
                                            ALU.not_equal).then_inc(edge_done, 1)
                for c, d in q.work("stats1", k):
                    q.wait(in_x1[c], 16, 16 * (d + 1))
                    statistics(q, h0[c], st1[c], mv1[c], st1_done, mv1_done, CH * d + c + 1)
                for c, d in q.work("stats2", k):
                    q.wait(x2_done, CH, CH * d + c + 1)
                    statistics(q, x2[c], st2[c], mv2[c], st2_done, mv2_done, CH * d + c + 1)
                for c, d in q.work("split2_lo", k):
                    q.wait(h2_hi_done, CH, CH * d + c + 1)
                    lo(h2_lo[c][:], h2[c % 2], h2_hi[c][:]).then_inc(h2_lo_done, 1)

            def body(q):
                for k in range(STEPS):
                    c_next, c_last = (k + 1) % CH, (k - 1) % CH
                    if q.least < 0:
                        weights(k)
                    if q.step(k + 1):
                        q.wait(t_hi, STEPS, k + 2)
                        if (k + 1) % STEPS < CH:
                            lo(h_lo[c_next][:], ps_t[:], h_hi[c_next][:]).then_inc(t_lo, 1)
                        else:
                            lo(n_lo[c_next][:].rearrange("p t d -> p (t d)"), ps_t[:],
                               n_hi[c_next][:].rearrange("p t d -> p (t d)")).then_inc(t_lo, 1)
                    if q.step(k - 1):
                        i = (k - 1) % 2
                        q.wait(n_done, STEPS, k)
                        nc.vector.scalar_tensor_tensor(cand[i][:], z_g[i][:], 1.0, cand[i][:],
                                                       ALU.subtract, ALU.mult).then_inc(zn_done, 1)
                        q.wait(zn_done, STEPS, k)
                        q.wait(zh_done, STEPS, k)
                        dst = h[c_last] if (k - 1) % STEPS < LAST else h_end[c_last]
                        nc.vector.tensor_tensor(dst[:], zh[i][:], cand[i][:], ALU.subtract).then_inc(h_done, 1)
                    for product in q.work("conv", k - 1):
                        leave(q, product)
                    if q.step(k):
                        q.wait(r_done, STEPS, k + 1)
                        nc.vector.scalar_tensor_tensor(cand[k % 2][:], ps_hn[k % 2][:], b_hh_cols[:, 2:3],
                                                       r_g[k % 2][:], ALU.add, ALU.mult).then_inc(rhn_done, 1)
                    if q.step(k + 1):
                        q.wait(p_split_hi, STEPS, k + 2)
                        lo(p_lo[(k + 1) % 2][:], ps_p[:], p_hi[(k + 1) % 2][:]).then_inc(p_split_lo, 1)
                    for product in q.work("conv_mid", k):
                        leave(q, product)
                    extras(q, k)
                    if q.step(k):
                        q.wait(gates_ready, STEPS, k + 1)
                        q.wait(rhn_done, STEPS, k + 1)
                        nc.vector.tensor_tensor(cand[k % 2][:], ps_in[:], cand[k % 2][:],
                                                ALU.add).then_inc(cand_done, 1)
                for product in q.work("conv", STEPS - 1):
                    leave(q, product)
                if q.least < 0:
                    last_weight()

            rounds(dve, body)

        @block.gpsimd
        def _(pool):
            nc.gpsimd.memset(ident[:], 0.0).then_inc(ident0, 1)
            nc.gpsimd.memset(minus_half[:], -0.5).then_inc(const_done, 1)
            nc.gpsimd.memset(eps[:], EPS).then_inc(const_done, 1)
            nc.gpsimd.memset(zero[:], 0.0).then_inc(const_done, 1)
            nc.gpsimd.memset(spare_act[:], 0.0).then_inc(const_done, 1)
            pool.wait_ge(ident0, 1)
            nc.gpsimd.affine_select(out=ident[:], in_=ident[:], compare_op=ALU.not_equal, fill=1.0, base=0,
                                    pattern=[[-1, P]], channel_multiplier=1).then_inc(ident_done, 1)
            pool.wait_ge(const_done, 4)

            def roots(q, mv, inv, n, added, rooted, count):
                nc.gpsimd.tensor_tensor(inv[:], mv[:, 1:n, :].rearrange("p s t -> p (s t)"),
                                        eps[:, 0:(n - 1) * T], ALU.add).then_inc(added, 1)
                q.wait(added, CH, count)
                nc.gpsimd.tensor_tensor(inv[:], inv[:], minus_half[:, 0:(n - 1) * T], ALU.pow).then_inc(rooted, 1)
                q.wait(rooted, CH, count)

            def shifts(q, shift, mv, scale, timed, done, count):
                nc.gpsimd.tensor_tensor(shift[:], mv[:, 0, :], scale, ALU.mult).then_inc(timed, 1)
                q.wait(timed, CH, count)
                nc.gpsimd.tensor_tensor(shift[:], zero[:], shift[:], ALU.subtract).then_inc(done, 1)

            def store_ready(q, product):
                kind, c, b, d = product
                if kind == "y" and not q.end:
                    q.wait(y_done, CH, CH * d + c + 1)
                    q.wait(x3_done, CH, CH * d + c + 1)
                    nc.gpsimd.tensor_tensor(x2[c][:], x2[c][:], h2[c % 2], ALU.add).then_inc(out_done, 1)

            def extras(q, k):
                for c, d in q.work("stats1", k):
                    q.wait(mv1_done, CH, CH * d + c + 1)
                    roots(q, mv1[c], inv1[c], 2, ve1_done, inv1_done, CH * d + c + 1)
                    shifts(q, shift1[c], mv1[c], inv1[c][:], mi1_done, shift1_done, CH * d + c + 1)
                for c, d in q.work("stats2", k):
                    q.wait(adj_summed, CH, CH * d + c + 1)
                    q.wait(mv2_done, CH, CH * d + c + 1)
                    roots(q, mv2[c], inv2[c], 3, ve2_done, inv2_done, CH * d + c + 1)
                    nc.gpsimd.tensor_tensor(inv2d[c][:], inv2[c][:, 0:T], inv2[c][:, T:2 * T],
                                            ALU.mult).then_inc(inv2d_done, 1)
                    q.wait(inv2d_done, CH, CH * d + c + 1)
                    shifts(q, shift2[c], mv2[c], inv2d[c][:], mi2_done, shift2_done, CH * d + c + 1)
                for c, d in q.work("bias", k):
                    q.wait(ln2_done, CH, CH * d + c + 1)
                    nc.gpsimd.tensor_tensor(x2[c][:], x2[c][:], b_out[:], ALU.add).then_inc(x3_done, 1)

            def body(q):
                busy = q.step(0)
                for k in range(STEPS):
                    c_next, c_last = (k + 1) % CH, (k - 1) % CH
                    if q.step(k + 1) and (k + 1) % STEPS < CH:
                        q.wait(t_lo, STEPS, k + 2)
                        nc.gpsimd.tensor_tensor(h[c_next][:], h_hi[c_next][:].bitcast(F32),
                                                h_lo[c_next][:].bitcast(F32), ALU.add).then_inc(h_first, 1)
                    if busy and k:
                        extras(q, k - 1)
                    for product in q.work("conv", k - 1):
                        store_ready(q, product)
                    if q.step(k - 1) and (k - 1) % STEPS < LAST:
                        q.wait(h_hi_done, LAST, k)
                        nc.gpsimd.tensor_tensor(h_lo[c_last][:], h[c_last][:], h_hi[c_last][:].bitcast(F32),
                                                ALU.subtract).then_inc(h_lo_done, 1)
                    if q.step(k + 2) and (k + 2) % STEPS < CH:
                        c = (k + 2) % CH
                        q.wait(n_hi_first, CH, (k + 2) // STEPS * CH + c + 1)
                        nc.gpsimd.tensor_tensor(n_lo[c][:], h0[c][:], n_hi[c][:].bitcast(F32),
                                                ALU.subtract).then_inc(n_lo_first, 1)
                    if not busy:
                        extras(q, k)
                    if q.step(k):
                        q.wait(z_done, STEPS, k + 1)
                        if k < CH:
                            q.wait(h_first, CH, k + 1)
                        nc.gpsimd.tensor_tensor(zh[k % 2][:], z_g[k % 2][:], h[k % CH][:],
                                                ALU.mult).then_inc(zh_done, 1)
                if busy:
                    extras(q, STEPS - 1)
                if q.least == 0:
                    pool.wait_ge(in_bias, 16 * T)
                for product in q.work("conv", STEPS - 1):
                    store_ready(q, product)

            rounds(pool, body)


_INS = ["x", "adj", "nodemask", "L0_gnn_weight", "L0_gnn_w_ih", "L0_gnn_w_hh", "L0_gnn_b_ih", "L0_gnn_b_hh",
        "L1_gnn_weight", "L1_gnn_bias"]


def kernel(**inputs):
    import numpy as _np
    import concourse.bacc as _bacc
    from concourse import mybir as _mybir
    from concourse.bass_utils import run_bass_kernel_spmd as _run

    nc = _bacc.Bacc("TRN2", target_bir_lowering=False, num_devices=1)
    arrays, args = {}, []
    for name in _INS:
        a = _np.ascontiguousarray(inputs[name])
        arrays[f"in_{name}"] = a
        args.append(nc.dram_tensor(f"in_{name}", a.shape, _mybir.dt.from_np(a.dtype), kind="ExternalInput").ap())
    shape = inputs["x"].shape
    out = nc.dram_tensor("out", shape, _mybir.dt.from_np(_np.dtype("float32")), kind="ExternalOutput").ap()
    build(nc, *args, out)
    return _run(nc, [arrays], core_ids=[0]).results[0]["out"]
```

```python
import concourse.bass as bass
from concourse import mybir
from contextlib import ExitStack


def build(nc, x, adj, nodemask, w_msg, w_ih, w_hh, b_ih, b_hh, w_conv, b_conv, out):
    F32 = mybir.dt.float32
    F32R = mybir.dt.float32r
    ALU = mybir.AluOpType
    ACT = mybir.ActivationFunctionType

    B, N, _ = x.shape
    L = w_msg.shape[0]
    P = 128
    K = N // P
    GB = 2
    T = GB * K
    COLS = T * P
    CH = 4
    ROUNDS = B // (GB * CH)
    STEPS = L * CH
    LAST = (L - 1) * CH
    ALL = STEPS * ROUNDS
    EPS = 1e-5
    NQ = 3

    x_v = x.rearrange("b n d -> (b n) d").rearrange("(g t p) d -> g p t d", t=T, p=P)
    out_v = out.rearrange("b n d -> (b n) d").rearrange("(g t p) d -> g p t d", t=T, p=P)
    adj_v = adj.rearrange("b n j -> (b n) j").rearrange("(g t p) j -> g p t j", t=T, p=P)

    ctx = ExitStack()
    with ctx:
        def sb(name, shape, dt=F32):
            return ctx.enter_context(nc.sbuf_tensor(name, shape, dt))

        def per_chain(name, shape, dt=F32, n=CH):
            return [sb(f"{name}{i}", shape, dt) for i in range(n)]

        def bank(name):
            return ctx.enter_context(nc.psum_tensor(name, [P, COLS], F32))

        def sem(name):
            return ctx.enter_context(nc.semaphore(name))

        ident = sb("ident", [P, P])
        minus_half = sb("minus_half", [P, T])
        eps = sb("eps", [P, T])
        zero = sb("zero", [P, T])
        w_conv_f = sb("w_conv_f", [P, P])
        n_mask_rows = B * K
        small_rows = sb("small_rows", [n_mask_rows + 2 * NQ, P])
        small_cols = sb("small_cols", [P, n_mask_rows + 2 * NQ])
        mask_cols = small_cols[:, 0:n_mask_rows]
        b_ih_cols = small_cols[:, n_mask_rows:n_mask_rows + NQ]
        b_hh_cols = small_cols[:, n_mask_rows + NQ:n_mask_rows + 2 * NQ]
        b_rz = sb("b_rz", [P, 2])
        b_out = sb("b_out", [P, T, P])
        u_hi = sb("u_hi", [P, L, NQ * P], F32R)
        u_lo = sb("u_lo", [P, L, NQ * P], F32R)
        v_hi = sb("v_hi", [P, NQ * P], F32R)
        v_lo = sb("v_lo", [P, NQ * P], F32R)
        c_hi = sb("c_hi", [P, P], F32R)
        c_lo = sb("c_lo", [P, P], F32R)

        h = per_chain("h", [P, COLS])
        h_hi = per_chain("h_hi", [P, COLS], F32R)
        h_lo = per_chain("h_lo", [P, COLS], F32R)
        h_end_all = sb("h_end_all", [P, CH * COLS])
        h_end = [h_end_all[:, c * COLS:(c + 1) * COLS] for c in range(CH)]
        n_hi = per_chain("n_hi", [P, T, P], F32R)
        n_lo = per_chain("n_lo", [P, T, P], F32R)
        edge = per_chain("edge", [P, T, N], F32R)
        h0 = per_chain("h0", [P, T, P])
        adj_a = per_chain("adj_a", [P, T, N], n=2)
        adj_b = per_chain("adj_b", [P, T, N])
        x2 = per_chain("x2", [P, T, P])
        h2_all = sb("h2_all", [P, 2 * COLS])
        h2 = [h2_all[:, i * COLS:(i + 1) * COLS].rearrange("p (t d) -> p t d", t=T) for i in range(2)]
        h2_hi = per_chain("h2_hi", [P, T, P], F32R)
        h2_lo = per_chain("h2_lo", [P, T, P], F32R)
        at_hi = per_chain("at_hi", [P, GB, K, N], F32R)
        at_lo = per_chain("at_lo", [P, GB, K, N], F32R)
        g_hi, g_lo = ([a[c][:, 1, :, :].rearrange("p k n -> p (k n)") for c in range(CH)] for a in (at_hi, at_lo))
        W3 = NQ * P
        w_ih_rows = h_end_all[:, 0:W3].rearrange("p (q e) -> p q e", q=NQ)
        w_hh_rows = h_end_all[:, W3:2 * W3].rearrange("p (q e) -> p q e", q=NQ)
        w_ih_t = h_end_all[:, 2 * W3:3 * W3]
        w_msg_rows = h_end_all[:, 3 * W3:3 * W3 + L * P].rearrange("p (l e) -> p l e", l=L)
        w_msg_t = h2_all[:, 0:L * P]
        p_hi = per_chain("p_hi", [P, COLS], F32R, n=2)
        p_lo = per_chain("p_lo", [P, COLS], F32R, n=2)
        r_g = per_chain("r_g", [P, COLS], n=2)
        z_g = per_chain("z_g", [P, COLS], n=2)
        cand = per_chain("cand", [P, COLS], n=2)
        zh = per_chain("zh", [P, COLS], n=2)
        st1 = per_chain("st1", [P, T, 6])
        st2 = per_chain("st2", [P, T, 6])
        mv1 = per_chain("mv1", [P, 2, T])
        mv2 = per_chain("mv2", [P, 2, T])
        spare, spare_act = sb("spare", [P, 1]), sb("spare_act", [P, 1])
        inv1 = per_chain("inv1", [P, T])
        inv2 = per_chain("inv2", [P, T])
        degree = per_chain("degree", [P, T])
        d2 = per_chain("d2", [P, T])
        inv2d = per_chain("inv2d", [P, T])
        shift1 = per_chain("shift1", [P, T])
        shift2 = per_chain("shift2", [P, T])

        ps_hn = [bank("ps_hn0"), bank("ps_hn1")]
        ps_r, ps_z, ps_in, ps_p, ps_t, ps_x = (bank(n) for n in ("ps_r", "ps_z", "ps_in", "ps_p", "ps_t", "ps_x"))

        u_banks = [ps_hn[0], ps_hn[1], ps_x]

        in_x1 = [sem(f"in_x1_{c}") for c in range(CH)]
        in_a1 = [sem(f"in_a1_{c}") for c in range(CH)]
        in_x2 = [sem(f"in_x2_{c}") for c in range(CH)]
        in_a2 = [sem(f"in_a2_{c}") for c in range(CH)]
        stored = [sem(f"stored_{c}") for c in range(CH)]
        in_w_ih, in_w_hh, in_msg, in_small, in_conv, in_bias = (
            sem(n) for n in ("in_w_ih", "in_w_hh", "in_msg", "in_small", "in_conv", "in_bias"))
        t_ready, p_ready, r_ready, z_ready, gates_ready = (
            sem(n) for n in ("t_ready", "p_ready", "r_ready", "z_ready", "gates_ready"))
        hend_t, adj_t, g_ready, y_ready = (sem(n) for n in ("hend_t", "adj_t", "g_ready", "y_ready"))
        t_hi, p_split_hi, r_done, z_done, n_done = (
            sem(n) for n in ("t_hi", "p_split_hi", "r_done", "z_done", "n_done"))
        h_hi_done = sem("h_hi_done")
        n_hi_first = sem("n_hi_first")
        h0_done, ln2_done, adj_summed = sem("h0_done"), sem("ln2_done"), sem("adj_summed")
        h2_hi_done, at_hi_done, g_hi_done, y_done = (
            sem(n) for n in ("h2_hi_done", "at_hi_done", "g_hi_done", "y_done"))
        t_lo, p_split_lo, rhn_done, cand_done, zn_done, h_done = (
            sem(n) for n in ("t_lo", "p_split_lo", "rhn_done", "cand_done", "zn_done", "h_done"))
        st1_done, mv1_done, edge_done = (
            sem(n) for n in ("st1_done", "mv1_done", "edge_done"))
        x2_done, st2_done, mv2_done, h2_lo_done, at_lo_done, g_lo_done = (
            sem(n) for n in ("x2_done", "st2_done", "mv2_done", "h2_lo_done", "at_lo_done", "g_lo_done"))
        zh_done = sem("zh_done")
        h_lo_done = sem("h_lo_done")
        h_first, n_lo_first, ve1_done, inv1_done, ve2_done, inv2_done, x3_done, out_done = (
            sem(n) for n in ("h_first", "n_lo_first", "ve1_done", "inv1_done", "ve2_done", "inv2_done",
                             "x3_done", "out_done"))
        de2_done, d2_done, inv2d_done = sem("de2_done"), sem("d2_done"), sem("inv2d_done")
        mi1_done, shift1_done, mi2_done, shift2_done = (
            sem(n) for n in ("mi1_done", "shift1_done", "mi2_done", "shift2_done"))
        ident0, ident_done, const_done = sem("ident0"), sem("ident_done"), sem("const_done")
        wt_ready, wt_act, wt_dve, u_ready, u_hi_done, u_lo_done = (
            sem(n) for n in ("wt_ready", "wt_act", "wt_dve", "u_ready", "u_hi_done", "u_lo_done"))

        def slots(at, d):
            out = {}
            for c, k in enumerate(at):
                out.setdefault(k, []).append((c, d))
            return out

        def joined(*parts):
            out = {}
            for part in parts:
                for k, work in part.items():
                    out.setdefault(k, []).extend(work)
            return out

        CONV = {k: [(p[0], int(p[1]), int(p[2]), -1)] for k, p in enumerate(
            "h00 a00 h10 a01 h20 a10 h30 a11 a20 a21 a30 a31 g00 g10 y00 g20 y10 g30 y20 y30".split())}

        def products(text):
            out = {}
            for word in text.split():
                k, p = word.split(":")
                out.setdefault(int(k), []).append((p[0], int(p[1]), int(p[2]), 0 if p.endswith("'") else -1))
            return out

        CONV_LAST = products("0:h00 1:a01 2:h10 3:a20 4:h20 5:a31 6:h30 7:g00 8:a00' 9:g10 10:y00 11:g20 "
                             "12:y10 13:g30 14:y20 15:y30 16:a30' 17:h00' 18:h10' 19:h20'")
        CONV_LAST_MID = products("1:a00 2:a10 3:a11 4:a21 5:a30 11:a01' 12:a10' 13:a11' 14:a20' 15:a21' 17:a31'")
        CONV_END = products("0:h30 2:g00 3:g10 4:g20 5:y00 6:g30 7:y10 8:y20 9:y30")

        STEADY = dict(
            conv=CONV, conv_mid={}, banks=[ps_x],
            sum_adj=slots([1, 2, 4, 6], -1), root_d=slots([1, 3, 5, 7], -1),
            stats2=slots([2, 4, 6, 8], -1), norm2=slots([3, 5, 7, 9], -1),
            split2=slots([4, 6, 8, 10], -1), split2_lo=slots([5, 7, 9, 11], -1), bias=slots([9, 10, 11, 12], -1),
            stats1=slots([12, 13, 15, 16], 1), norm1=slots([13, 14, 16, 17], 1), edges=slots([17, 17, 18, 19], 1))
        START = dict(STEADY, stats1=slots([14, 15, 18, 19], 1), norm1=slots([17, 18, 19], 1),
                     edges=slots([17, 18], 1))
        FIRST = dict(STEADY, stats1=slots([7, 9, 11, 13], 1), norm1=joined(slots([8, 10, 12, 14], 1), {0: [(3, 0)]}),
                     edges=joined(STEADY["edges"], {0: [(2, 0)], 1: [(3, 0)]}))
        own = dict(sum_adj=slots([8, 10, 12, 14], 0), root_d=slots([11, 13, 15, 17], 0),
                   stats2=slots([18, 19], 0))
        LAST_ROUND = dict(STEADY, sum_adj=slots([0, 1, 2, 4], -1))
        LAST_ROUND.update({name: joined(LAST_ROUND[name], at) for name, at in own.items()},
                          conv=CONV_LAST, conv_mid=CONV_LAST_MID)
        END = dict(STEADY, conv=CONV_END, banks=[ps_x, ps_r, ps_z, ps_in], sum_adj={}, root_d={},
                   stats2={0: [(2, -1)], 1: [(3, -1)]}, norm2=slots([0, 1, 2, 3], -1), split2=slots([0, 1, 2, 3], -1),
                   split2_lo=slots([0, 2, 2, 3], -1), bias=slots([3, 3, 4, 5], -1))

        class Round:

            def __init__(self, eng, r, first=None, last=None):
                self.eng, self.r = eng, r
                self.least, self.most = (r, r) if first is None else (first, last)
                self.base, self.counts, self.seen = {}, {}, {}
                self.end = self.least == ROUNDS
                self.plan = {-1: START, 0: FIRST, ROUNDS - 1: LAST_ROUND, ROUNDS: END}.get(self.least, STEADY)
                self.products = [p for k in range(STEPS)
                                 for p in self.work("conv_mid", k) + self.work("conv", k)]

            def work(self, name, k):
                return [w for w in self.plan[name].get(k, []) if self.group(w[-1])]

            def bank(self, product):
                banks = self.plan["banks"]
                return banks[self.products.index(product) % len(banks)]

            def before(self, product):
                i = self.products.index(product) - len(self.plan["banks"])
                return self.products[i] if i >= 0 else None

            def step(self, k):
                return 0 <= self.least * STEPS + k and self.most * STEPS + k < ALL

            def group(self, d):
                return 0 <= self.least + d and self.most + d < ROUNDS

            def value(self, per_round, count):
                if isinstance(self.r, int):
                    return self.r * per_round + count
                assert self.least * per_round + count > 0, (per_round, count)
                if per_round not in self.base:
                    self.base[per_round] = self.eng.snap(self.r * per_round)
                key = per_round, count
                if key not in self.counts:
                    self.counts = {key: self.eng.snap(self.base[per_round] + count)}
                return self.counts[key]

            def wait(self, s, per_round, count):
                if self.most * per_round + count > 0 and count > self.seen.get(id(s), (s, count - 1))[1]:
                    self.seen[id(s)] = s, count
                    self.eng.wait_ge(s, self.value(per_round, count))

        UNITS = [15, 16, 18, 18, 18]

        def rounds(eng, body):
            body(Round(eng, -1))
            body(Round(eng, 0))
            with eng.Fori(1, ROUNDS - 1) as r:
                body(Round(eng, r, 1, ROUNDS - 2))
            body(Round(eng, ROUNDS - 1))
            body(Round(eng, ROUNDS))

        block = ctx.enter_context(nc.Block())

        @block.sync
        def _(sp):
            sp.dma_start(w_ih_rows, w_ih.rearrange("(q p) e -> p q e", p=P)).then_inc(in_w_ih, 16)
            sp.dma_start(w_msg_rows, w_msg.rearrange("l d e -> d l e")).then_inc(in_msg, 16)

            def body(q):
                r = q.r
                if q.group(+1):
                    for c in range(CH):
                        q.wait(h_first, CH, c + 1)
                        sp.dma_start(h0[c][:], x_v[(r + 1) * CH + c]).then_inc(in_x1[c], 16)
                        if q.least == -1 and c == 0:
                            sp.dma_start(w_hh_rows, w_hh.rearrange("(q p) e -> p q e", p=P)).then_inc(in_w_hh, 16)
                            sp.dma_start(small_rows[0:n_mask_rows, :],
                                         nodemask.rearrange("b (k p) -> (b k) p", p=P)).then_inc(in_small, 16)
                            sp.dma_start(small_rows[n_mask_rows:n_mask_rows + NQ, :],
                                         b_ih.rearrange("(q p) -> q p", p=P)).then_inc(in_small, 16)
                            sp.dma_start(small_rows[n_mask_rows + NQ:n_mask_rows + 2 * NQ, :],
                                         b_hh.rearrange("(q p) -> q p", p=P)).then_inc(in_small, 16)
                        if q.least == -1 and c == 1:
                            sp.dma_start(w_conv_f[:], w_conv).then_inc(in_conv, 16)
                        if c in (1, 2):
                            q.wait(edge_done, CH, CH + c - 2)
                            sp.dma_start(adj_a[c - 1][:], adj_v[(r + 1) * CH + c - 1]).then_inc(in_a1[c - 1], 16)
                if q.least == -1:
                    for t in range(T):
                        sp.dma_start(b_out[:, t, :],
                                     b_conv.rearrange("(o d) -> o d", o=1).broadcast_to((P, P))).then_inc(in_bias, 16)
                if q.group(0):
                    for c in range(CH):
                        q.wait(at_lo_done, GB * CH, -GB * CH + GB * (c + 1))
                        sp.dma_start(adj_b[c][:], adj_v[r * CH + c]).then_inc(in_a2[c], 16)
                if q.group(+1):
                    for c in range(2, CH):
                        q.wait(edge_done, CH, CH + c - 1)
                        sp.dma_start(adj_a[c - 2][:], adj_v[(r + 1) * CH + c]).then_inc(in_a1[c], 16)
                for c in range(CH + 1):
                    if q.group(-1) and c < CH:
                        q.wait(out_done, CH, -CH + c + 1)
                        sp.dma_start(out_v[(r - 1) * CH + c], x2[c][:]).then_inc(stored[c], 16)
                    if q.group(0) and c > 0:
                        q.wait(stored[c - 1], 16, 0)
                        sp.dma_start(x2[c - 1][:], x_v[r * CH + c - 1]).then_inc(in_x2[c - 1], 16)

            rounds(sp, body)
            for c in range(CH):
                sp.wait_ge(stored[c], 16 * ROUNDS)

        @block.tensor
        def _(pe):
            pe.wait_ge(ident_done, 1)
            pe.wait_ge(in_w_ih, 16)
            for i in range(NQ):
                last = nc.tensor.transpose(ps_r[:, i * P:(i + 1) * P], w_ih_rows[:, i, :], ident[:])
            last.then_inc(wt_ready, 1)
            pe.wait_ge(in_msg, 16)
            for l in range(L):
                ps = ps_in if l < 4 else ps_p
                last = nc.tensor.transpose(ps[:, l % 4 * P:(l % 4 + 1) * P], w_msg_rows[:, l, :], ident[:])
            last.then_inc(wt_ready, 1)
            pe.wait_ge(in_w_hh, 16)
            for i in range(NQ):
                last = nc.tensor.transpose(ps_z[:, i * P:(i + 1) * P], w_hh_rows[:, i, :], ident[:])
            last.then_inc(wt_ready, 1)

            def unite(l):
                if l >= len(u_banks):
                    pe.wait_ge(u_lo_done, l - len(u_banks) + 1)
                nc.tensor.matmul(u_banks[l % len(u_banks)][:, 0:NQ * P], w_msg_t[:, l * P:(l + 1) * P], w_ih_t,
                                 start=True, stop=True).then_inc(u_ready, 1)

            pe.wait_ge(wt_act, 1)
            pe.wait_ge(wt_dve, 1)
            for l in range(2):
                unite(l)
            pe.wait_ge(in_small, 48)
            n = n_mask_rows + 2 * NQ
            nc.tensor.transpose(ps_t[:, 0:n], small_rows[:], ident[0:n, 0:n]).then_inc(wt_ready, 1)
            for l in range(2, L - 1):
                unite(l)

            def mm3(o, w_hi, w_lo, m_hi, m_lo, start, stop):
                nc.tensor.matmul(o, w_hi, m_hi, start=start, stop=False)
                nc.tensor.matmul(o, w_hi, m_lo, start=False, stop=False)
                return nc.tensor.matmul(o, w_lo, m_hi, start=False, stop=stop)

            def gate_h(o, i, c, stop):
                w = slice(i * P, (i + 1) * P)
                return mm3(o[:], v_hi[:, w], v_lo[:, w], h_hi[c][:], h_lo[c][:], True, stop)

            def gate_m(o, i, l, k, start):
                w = slice(i * P, (i + 1) * P)
                return mm3(o[:], u_hi[:, l, w], u_lo[:, l, w], p_hi[k % 2][:], p_lo[k % 2][:], start, True)

            def hn_and_r(q, k):
                l, c = k // CH, k % CH
                if l:
                    q.wait(h_hi_done, LAST, k - CH + 1)
                    q.wait(h_lo_done, LAST, k - CH + 1)
                else:
                    q.wait(t_hi, STEPS, k + 1)
                    q.wait(t_lo, STEPS, k + 1)
                q.wait(rhn_done, STEPS, k - 1)
                gate_h(ps_hn[k % 2], 2, c, True)
                q.wait(r_done, STEPS, k)
                gate_h(ps_r, 0, c, False)
                q.wait(p_split_hi, STEPS, k + 1)
                q.wait(p_split_lo, STEPS, k + 1)
                gate_m(ps_r, 0, l, k, False).then_inc(r_ready, 1)

            def z_and_in(q, k):
                l, c = k // CH, k % CH
                q.wait(z_done, STEPS, k)
                gate_h(ps_z, 1, c, False)
                gate_m(ps_z, 1, l, k, False).then_inc(z_ready, 1)
                q.wait(cand_done, STEPS, k)
                gate_m(ps_in, 2, l, k, True).then_inc(gates_ready, 1)

            def aggregate(q, k):
                c = k % CH
                if k % STEPS < CH:
                    e = k // STEPS * CH + c + 1
                    q.wait(n_hi_first, CH, e)
                    q.wait(n_lo_first, CH, e)
                    q.wait(edge_done, CH, e)
                else:
                    q.wait(t_hi, STEPS, k + 1)
                    q.wait(t_lo, STEPS, k + 1)
                q.wait(p_split_hi, STEPS, k)
                q.wait(p_split_lo, STEPS, k)
                for b in range(GB):
                    for i in range(K):
                        t = b * K + i
                        o = ps_p[:, b * N:(b + 1) * N]
                        nc.tensor.matmul(o, n_hi[c][:, t, :], edge[c][:, t, :], start=(i == 0), stop=False)
                        last = nc.tensor.matmul(o, n_lo[c][:, t, :], edge[c][:, t, :],
                                                start=False, stop=(i == K - 1))
                last.then_inc(p_ready, 1)

            def transposes(q, k):
                c = k % CH
                if k % STEPS < CH:
                    q.wait(h0_done, CH, k // STEPS * CH + c + 1)
                else:
                    q.wait(h_done, STEPS, k - CH + 1)
                q.wait(t_hi, STEPS, k)
                q.wait(t_lo, STEPS, k)
                for t in range(T):
                    src = h0[c][:, t, :] if k % STEPS < CH else h[c][:, t * P:(t + 1) * P]
                    last = nc.tensor.transpose(ps_t[:, t * P:(t + 1) * P], src, ident[:])
                last.then_inc(t_ready, 1)

            def has_left(q, product):
                kind, c, b, d = product
                if kind == "h":
                    q.wait(x2_done, CH, CH * d + c + 1)
                elif kind == "a":
                    q.wait(at_hi_done, GB * CH, GB * (CH * d + c) + b + 1)
                    q.wait(at_lo_done, GB * CH, GB * (CH * d + c) + b + 1)
                elif kind == "g":
                    q.wait(g_hi_done, CH, CH * d + c + 1)
                    q.wait(g_lo_done, CH, CH * d + c + 1)
                else:
                    q.wait(out_done if q.end else y_done, CH, CH * d + c + 1)

            def second_conv(q, product):
                kind, c, b, d = product
                if q.before(product):
                    has_left(q, q.before(product))
                elif q.end:
                    q.wait(x2_done, CH, 3 - CH)
                    q.wait(z_done, STEPS, 0)
                    q.wait(cand_done, STEPS, 0)
                else:
                    q.wait(n_done, STEPS, 0)
                ps = q.bank(product)
                if kind == "h":
                    q.wait(h_done, STEPS, STEPS * d + LAST + c + 1)
                    for t in range(T):
                        last = nc.tensor.transpose(ps[:, t * P:(t + 1) * P],
                                                   h_end[c][:, t * P:(t + 1) * P], ident[:])
                    last.then_inc(hend_t, 1)
                elif kind == "a":
                    q.wait(in_a2[c], 16, 16 * (d + 1))
                    for i in range(K):
                        for n in range(K):
                            last = nc.tensor.transpose(
                                ps[:, i * N + n * P:i * N + (n + 1) * P],
                                adj_b[c][:, b * K + n, i * P:(i + 1) * P], ident[:])
                    last.then_inc(adj_t, 1)
                elif kind == "g":
                    q.wait(h2_hi_done, CH, CH * d + c + 1)
                    q.wait(h2_lo_done, CH, CH * d + c + 1)
                    q.wait(at_hi_done, GB * CH, GB * (CH * d + c + 1))
                    q.wait(at_lo_done, GB * CH, GB * (CH * d + c + 1))
                    for b in range(GB):
                        for i in range(K):
                            last = mm3(ps[:, b * N:(b + 1) * N],
                                       h2_hi[c][:, b * K + i, :], h2_lo[c][:, b * K + i, :],
                                       at_hi[c][:, b, i, :], at_lo[c][:, b, i, :], i == 0, i == K - 1)
                    last.then_inc(g_ready, 1)
                else:
                    q.wait(g_hi_done, CH, CH * d + c + 1)
                    q.wait(g_lo_done, CH, CH * d + c + 1)
                    for t in range(T):
                        w = slice(t * P, (t + 1) * P)
                        last = mm3(ps[:, w], g_hi[c][:, w], g_lo[c][:, w], c_hi[:], c_lo[:], True, True)
                    last.then_inc(y_ready, 1)

            pe.wait_ge(wt_dve, 3)

            def body(q):
                if q.least == 0:
                    pe.wait_ge(u_hi_done, L)
                    pe.wait_ge(u_lo_done, L)
                for k in range(STEPS):
                    if q.least < 0 and k == STEPS - 1:
                        unite(L - 1)
                    if q.step(k):
                        hn_and_r(q, k)
                    if q.step(k + 1):
                        aggregate(q, k + 1)
                    if q.step(k + 2):
                        transposes(q, k + 2)
                    for product in q.work("conv_mid", k):
                        second_conv(q, product)
                    if q.step(k):
                        z_and_in(q, k)
                    for product in q.work("conv", k):
                        second_conv(q, product)

                if q.least == 0:
                    pe.wait_ge(wt_act, 3)
                    pe.wait_ge(wt_dve, 5)

            rounds(pe, body)

        @block.scalar
        def _(act):
            act.wait_ge(const_done, 4)
            nc.scalar.activation(spare_act[:], spare_act[:], ACT.Sigmoid)
            act.wait_ge(wt_ready, 2)
            nc.scalar.activation(w_msg_t[:, 0:COLS], ps_in[:], ACT.Copy)
            nc.scalar.activation(w_msg_t[:, COLS:L * P], ps_p[:, 0:L * P - COLS], ACT.Copy).then_inc(wt_act, 1)
            act.wait_ge(wt_ready, 3)
            nc.scalar.activation(v_hi[:], ps_z[:, 0:NQ * P], ACT.Copy).then_inc(wt_act, 1)

            def weights(k):
                for l in range(L):
                    if UNITS[l] == k:
                        act.wait_ge(u_ready, l + 1)
                        nc.scalar.activation(u_hi[:, l, :], u_banks[l % len(u_banks)][:, 0:NQ * P],
                                             ACT.Copy).then_inc(u_hi_done, 1)
                if k == STEPS - 1:
                    act.wait_ge(in_conv, 16)
                    nc.scalar.activation(c_hi[:], w_conv_f[:], ACT.Copy).then_inc(wt_act, 1)
                    act.wait_ge(wt_dve, 4)

            def hi(dst, src):
                return nc.scalar.activation(dst, src, ACT.Copy)

            def leave(q, product):
                kind, c, b, d = product
                ps = q.bank(product)
                if kind == "a":
                    q.wait(adj_t, GB * CH, GB * (CH * d + c) + b + 1)
                    hi(at_hi[c][:, b, :, :].rearrange("p k n -> p (k n)"), ps[:]).then_inc(at_hi_done, 1)
                elif kind == "g":
                    q.wait(g_ready, CH, CH * d + c + 1)
                    hi(g_hi[c], ps[:]).then_inc(g_hi_done, 1)
                elif kind == "y":
                    if not q.end:
                        q.wait(y_ready, CH, CH * d + c + 1)
                        q.wait(d2_done, CH, CH * d + c + 1)
                        q.wait(h2_lo_done, CH, CH * d + min(c + 3, CH))
                        if c >= 2:
                            q.wait(out_done, CH, CH * d + c - 1)
                        for t in range(T):
                            last = nc.scalar.activation(h2[c % 2][:, t, :], ps[:, t * P:(t + 1) * P], ACT.Copy,
                                                        scale=d2[c][:, t:t + 1])
                        last.then_inc(y_done, 1)

            def first_hi(q, k):
                if q.step(k) and k % STEPS < CH:
                    c = k % CH
                    q.wait(h0_done, CH, k // STEPS * CH + c + 1)
                    q.wait(p_ready, STEPS, k + 1 - CH)
                    hi(n_hi[c][:], h0[c][:]).then_inc(n_hi_first, 1)

            def sum_adj(q, c, d):
                q.wait(in_a2[c], 16, 16 * (d + 1))
                for t in range(T):
                    unused = (h2_hi, h2_lo)[t // 2][c][:].rearrange("p t d -> p (t d)")[:, t % 2 * N:(t % 2 + 1) * N]
                    last = nc.scalar.activation(unused, adj_b[c][:, t, :],
                                                ACT.Copy, accum_out=degree[c][:, t:t + 1])
                last.then_inc(adj_summed, 1)

            def norm(dst, src, inv, shift):
                for t in range(T):
                    last = nc.scalar.activation(dst[:, t, :], src[:, t, :], ACT.Relu,
                                                bias=shift[:, t:t + 1], scale=inv[:, t:t + 1])
                return last

            def body(q):
                for k in range(STEPS):
                    for product in q.work("conv", k - 1):
                        leave(q, product)
                    if q.step(k - 1):
                        q.wait(cand_done, STEPS, k)
                        nc.scalar.activation(cand[(k - 1) % 2][:], cand[(k - 1) % 2][:], ACT.Tanh,
                                             bias=b_ih_cols[:, 2:3]).then_inc(n_done, 1)
                    if q.step(k):
                        q.wait(r_ready, STEPS, k + 1)
                        q.wait(rhn_done, STEPS, k - 1)
                        nc.scalar.activation(r_g[k % 2][:], ps_r[:], ACT.Sigmoid,
                                             bias=b_rz[:, 0:1]).then_inc(r_done, 1)
                    if q.step(k + 1):
                        q.wait(p_ready, STEPS, k + 2)
                        q.wait(gates_ready, STEPS, k)
                        hi(p_hi[(k + 1) % 2][:], ps_p[:]).then_inc(p_split_hi, 1)
                    for product in q.work("conv_mid", k):
                        leave(q, product)
                    if q.least < 0:
                        first_hi(q, k + 2)
                    if q.step(k + 2):
                        c = (k + 2) % CH
                        q.wait(t_ready, STEPS, k + 3)
                        if (k + 2) % STEPS < CH:
                            q.wait(gates_ready, STEPS, k + 3 - CH)
                            hi(h_hi[c][:], ps_t[:]).then_inc(t_hi, 1)
                        else:
                            q.wait(p_ready, STEPS, k + 3 - CH)
                            hi(n_hi[c][:].rearrange("p t d -> p (t d)"), ps_t[:]).then_inc(t_hi, 1)
                    if q.step(k - 1) and (k - 1) % STEPS < LAST:
                        q.wait(h_done, STEPS, k)
                        q.wait(gates_ready, STEPS, k)
                        hi(h_hi[(k - 1) % CH][:], h[(k - 1) % CH][:]).then_inc(h_hi_done, 1)
                    if q.least >= 0:
                        first_hi(q, k + 2)
                    if q.least < 0:
                        weights(k)
                    for c, d in q.work("norm1", k):
                        q.wait(shift1_done, CH, CH * d + c + 1)
                        norm(h0[c], h0[c], inv1[c], shift1[c]).then_inc(h0_done, 1)
                    for c, d in q.work("norm2", k):
                        q.wait(shift2_done, CH, CH * d + c + 1)
                        q.wait(x2_done, CH, CH * d + c + 1)
                        if c >= 2:
                            q.wait(h2_lo_done, CH, CH * d + c - 1)
                        norm(h2[c % 2], x2[c], inv2d[c], shift2[c]).then_inc(ln2_done, 1)
                    for c, d in q.work("split2", k):
                        q.wait(ln2_done, CH, CH * d + c + 1)
                        hi(h2_hi[c][:], h2[c % 2]).then_inc(h2_hi_done, 1)
                    for c, d in q.work("sum_adj", k):
                        sum_adj(q, c, d)
                    if q.step(k):
                        q.wait(z_ready, STEPS, k + 1)
                        q.wait(zn_done, STEPS, k - 1)
                        q.wait(zh_done, STEPS, k - 1)
                        nc.scalar.activation(z_g[k % 2][:], ps_z[:], ACT.Sigmoid,
                                             bias=b_rz[:, 1:2]).then_inc(z_done, 1)
                for product in q.work("conv", STEPS - 1):
                    leave(q, product)

            rounds(act, body)

        @block.vector
        def _(dve):
            dve.wait_ge(wt_ready, 1)
            nc.vector.tensor_copy(w_ih_t, ps_r[:, 0:NQ * P]).then_inc(wt_dve, 1)

            def weights(k):
                if k == UNITS[0]:
                    dve.wait_ge(wt_act, 2)
                    nc.vector.tensor_tensor(v_lo[:], ps_z[:, 0:NQ * P], v_hi[:].bitcast(F32),
                                            ALU.subtract).then_inc(wt_dve, 1)
                for l in range(L):
                    if UNITS[l] == k:
                        dve.wait_ge(u_hi_done, l + 1)
                        nc.vector.tensor_tensor(u_lo[:, l, :], u_banks[l % len(u_banks)][:, 0:NQ * P],
                                                u_hi[:, l, :].bitcast(F32), ALU.subtract).then_inc(u_lo_done, 1)
                if k == UNITS[1]:
                    dve.wait_ge(wt_ready, 4)
                    nc.vector.tensor_copy(small_cols[:], ps_t[:, 0:n_mask_rows + 2 * NQ]).then_inc(wt_dve, 1)
                    dve.wait_ge(wt_dve, 3)
                    nc.vector.tensor_tensor(b_rz[:], b_ih_cols[:, 0:2], b_hh_cols[:, 0:2],
                                            ALU.add).then_inc(wt_dve, 1)

            def last_weight():
                dve.wait_ge(wt_act, 3)
                nc.vector.tensor_tensor(c_lo[:], w_conv_f[:], c_hi[:].bitcast(F32), ALU.subtract).then_inc(wt_dve, 1)

            def lo(dst, src, part):
                return nc.vector.tensor_tensor(dst, src, part.bitcast(F32), ALU.subtract)

            def statistics(q, src, st, mv, st_done, mv_done, count):
                for t in range(T):
                    last = nc.vector.bn_stats(st[:, t, :], src[:, t, :])
                last.then_inc(st_done, 1)
                q.wait(st_done, CH, count)
                nc.vector.memset(spare[:], 0.0)
                for t in range(T):
                    last = nc.vector.bn_aggr(mv[:, 0:2, t], st[:, t, :])
                last.then_inc(mv_done, 1)

            def leave(q, product):
                kind, c, b, d = product
                ps = q.bank(product)
                if kind == "h":
                    q.wait(hend_t, CH, CH * d + c + 1)
                    q.wait(in_x2[c], 16, 16 * (d + 1))
                    for t in range(T):
                        col = ((q.r + d) * CH + c) * T + t
                        last = nc.vector.scalar_tensor_tensor(
                            x2[c][:, t, :], ps[:, t * P:(t + 1) * P], mask_cols[:, bass.ds(col, 1)],
                            x2[c][:, t, :], ALU.mult, ALU.add)
                    last.then_inc(x2_done, 1)
                elif kind == "a":
                    q.wait(at_hi_done, GB * CH, GB * (CH * d + c) + b + 1)
                    lo(at_lo[c][:, b, :, :].rearrange("p k n -> p (k n)"), ps[:],
                       at_hi[c][:, b, :, :].rearrange("p k n -> p (k n)")).then_inc(at_lo_done, 1)
                elif kind == "g":
                    q.wait(g_hi_done, CH, CH * d + c + 1)
                    lo(g_lo[c], ps[:], g_hi[c]).then_inc(g_lo_done, 1)
                elif q.end:
                    q.wait(y_ready, CH, CH * d + c + 1)
                    q.wait(x3_done, CH, CH * d + c + 1)
                    for t in range(T):
                        last = nc.vector.scalar_tensor_tensor(
                            x2[c][:, t, :], ps[:, t * P:(t + 1) * P], d2[c][:, t:t + 1],
                            x2[c][:, t, :], ALU.mult, ALU.add)
                    last.then_inc(out_done, 1)

            def extras(q, k):
                for c, d in q.work("edges", k):
                    q.wait(in_a1[c], 16, 16 * (d + 1))
                    q.wait(p_ready, STEPS, STEPS * (d - 1) + LAST + c + 1)
                    nc.vector.tensor_scalar(edge[c][:], adj_a[c % 2][:], 0.0, None,
                                            ALU.not_equal).then_inc(edge_done, 1)
                for c, d in q.work("stats1", k):
                    q.wait(in_x1[c], 16, 16 * (d + 1))
                    statistics(q, h0[c], st1[c], mv1[c], st1_done, mv1_done, CH * d + c + 1)
                for c, d in q.work("split2_lo", k):
                    q.wait(h2_hi_done, CH, CH * d + c + 1)
                    lo(h2_lo[c][:], h2[c % 2], h2_hi[c][:]).then_inc(h2_lo_done, 1)
                for c, d in q.work("stats2", k):
                    q.wait(x2_done, CH, CH * d + c + 1)
                    statistics(q, x2[c], st2[c], mv2[c], st2_done, mv2_done, CH * d + c + 1)

            def body(q):
                for k in range(STEPS):
                    c_last = (k - 1) % CH
                    for product in q.work("conv", k - 1):
                        leave(q, product)
                    if q.step(k - 1):
                        i = (k - 1) % 2
                        q.wait(n_done, STEPS, k)
                        nc.vector.scalar_tensor_tensor(cand[i][:], z_g[i][:], 1.0, cand[i][:],
                                                       ALU.subtract, ALU.mult).then_inc(zn_done, 1)
                        q.wait(zn_done, STEPS, k)
                        q.wait(zh_done, STEPS, k)
                        dst = h[c_last] if (k - 1) % STEPS < LAST else h_end[c_last]
                        nc.vector.tensor_tensor(dst[:], zh[i][:], cand[i][:], ALU.subtract).then_inc(h_done, 1)
                    if q.step(k):
                        q.wait(r_done, STEPS, k + 1)
                        nc.vector.scalar_tensor_tensor(cand[k % 2][:], ps_hn[k % 2][:], b_hh_cols[:, 2:3],
                                                       r_g[k % 2][:], ALU.add, ALU.mult).then_inc(rhn_done, 1)
                    if q.step(k + 1):
                        q.wait(p_split_hi, STEPS, k + 2)
                        lo(p_lo[(k + 1) % 2][:], ps_p[:], p_hi[(k + 1) % 2][:]).then_inc(p_split_lo, 1)
                    for product in q.work("conv_mid", k):
                        leave(q, product)
                    if q.least < 0 and k >= STEPS - 2:
                        c = (k + 2) % CH
                        q.wait(n_hi_first, CH, CH + c + 1)
                        lo(n_lo[c][:], h0[c][:], n_hi[c][:]).then_inc(n_lo_first, 1)
                    if q.step(k + 2):
                        c = (k + 2) % CH
                        q.wait(t_hi, STEPS, k + 3)
                        if (k + 2) % STEPS < CH:
                            lo(h_lo[c][:], ps_t[:], h_hi[c][:]).then_inc(t_lo, 1)
                        else:
                            lo(n_lo[c][:].rearrange("p t d -> p (t d)"), ps_t[:],
                               n_hi[c][:].rearrange("p t d -> p (t d)")).then_inc(t_lo, 1)
                    if q.least < 0:
                        weights(k)
                    extras(q, k)
                    if q.step(k):
                        q.wait(gates_ready, STEPS, k + 1)
                        q.wait(rhn_done, STEPS, k + 1)
                        nc.vector.tensor_tensor(cand[k % 2][:], ps_in[:], cand[k % 2][:],
                                                ALU.add).then_inc(cand_done, 1)
                for product in q.work("conv", STEPS - 1):
                    leave(q, product)
                if q.least < 0:
                    last_weight()

            rounds(dve, body)

        @block.gpsimd
        def _(pool):
            nc.gpsimd.memset(ident[:], 0.0).then_inc(ident0, 1)
            nc.gpsimd.memset(minus_half[:], -0.5).then_inc(const_done, 1)
            nc.gpsimd.memset(eps[:], EPS).then_inc(const_done, 1)
            nc.gpsimd.memset(zero[:], 0.0).then_inc(const_done, 1)
            nc.gpsimd.memset(spare_act[:], 0.0).then_inc(const_done, 1)
            pool.wait_ge(ident0, 1)
            nc.gpsimd.affine_select(out=ident[:], in_=ident[:], compare_op=ALU.not_equal, fill=1.0, base=0,
                                    pattern=[[-1, P]], channel_multiplier=1).then_inc(ident_done, 1)
            pool.wait_ge(const_done, 4)

            def root(q, src, dst, added, rooted, count):
                nc.gpsimd.tensor_tensor(dst[:], src, eps[:], ALU.add).then_inc(added, 1)
                q.wait(added, CH, count)
                nc.gpsimd.tensor_tensor(dst[:], dst[:], minus_half[:], ALU.pow).then_inc(rooted, 1)
                q.wait(rooted, CH, count)

            def shifts(q, shift, mv, scale, timed, done, count):
                nc.gpsimd.tensor_tensor(shift[:], mv[:, 0, :], scale, ALU.mult).then_inc(timed, 1)
                q.wait(timed, CH, count)
                nc.gpsimd.tensor_tensor(shift[:], zero[:], shift[:], ALU.subtract).then_inc(done, 1)

            def store_ready(q, product):
                kind, c, b, d = product
                if kind == "y" and not q.end:
                    q.wait(y_done, CH, CH * d + c + 1)
                    q.wait(x3_done, CH, CH * d + c + 1)
                    nc.gpsimd.tensor_tensor(x2[c][:], x2[c][:], h2[c % 2], ALU.add).then_inc(out_done, 1)

            def extras(q, k):
                for c, d in q.work("stats1", k):
                    q.wait(mv1_done, CH, CH * d + c + 1)
                    root(q, mv1[c][:, 1, :], inv1[c], ve1_done, inv1_done, CH * d + c + 1)
                    shifts(q, shift1[c], mv1[c], inv1[c][:], mi1_done, shift1_done, CH * d + c + 1)
                for c, d in q.work("root_d", k):
                    q.wait(adj_summed, CH, CH * d + c + 1)
                    root(q, degree[c][:], d2[c], de2_done, d2_done, CH * d + c + 1)
                for c, d in q.work("stats2", k):
                    q.wait(d2_done, CH, CH * d + c + 1)
                    q.wait(mv2_done, CH, CH * d + c + 1)
                    root(q, mv2[c][:, 1, :], inv2[c], ve2_done, inv2_done, CH * d + c + 1)
                    nc.gpsimd.tensor_tensor(inv2d[c][:], inv2[c][:], d2[c][:],
                                            ALU.mult).then_inc(inv2d_done, 1)
                    q.wait(inv2d_done, CH, CH * d + c + 1)
                    shifts(q, shift2[c], mv2[c], inv2d[c][:], mi2_done, shift2_done, CH * d + c + 1)
                for c, d in q.work("bias", k):
                    q.wait(ln2_done, CH, CH * d + c + 1)
                    nc.gpsimd.tensor_tensor(x2[c][:], x2[c][:], b_out[:], ALU.add).then_inc(x3_done, 1)

            def body(q):
                busy = q.step(0)
                for k in range(STEPS):
                    c_next, c_last = (k + 1) % CH, (k - 1) % CH
                    if q.step(k + 1) and (k + 1) % STEPS < CH:
                        q.wait(t_lo, STEPS, k + 2)
                        nc.gpsimd.tensor_tensor(h[c_next][:], h_hi[c_next][:].bitcast(F32),
                                                h_lo[c_next][:].bitcast(F32), ALU.add).then_inc(h_first, 1)
                    if busy and k:
                        extras(q, k - 1)
                    for product in q.work("conv", k - 1):
                        store_ready(q, product)
                    if q.step(k - 1) and (k - 1) % STEPS < LAST:
                        q.wait(h_hi_done, LAST, k)
                        nc.gpsimd.tensor_tensor(h_lo[c_last][:], h[c_last][:], h_hi[c_last][:].bitcast(F32),
                                                ALU.subtract).then_inc(h_lo_done, 1)
                    if q.least >= 0 and q.step(k + 2) and (k + 2) % STEPS < CH:
                        c = (k + 2) % CH
                        q.wait(n_hi_first, CH, (k + 2) // STEPS * CH + c + 1)
                        nc.gpsimd.tensor_tensor(n_lo[c][:], h0[c][:], n_hi[c][:].bitcast(F32),
                                                ALU.subtract).then_inc(n_lo_first, 1)
                    if not busy:
                        extras(q, k)
                    if q.step(k):
                        q.wait(z_done, STEPS, k + 1)
                        if k < CH:
                            q.wait(h_first, CH, k + 1)
                        nc.gpsimd.tensor_tensor(zh[k % 2][:], z_g[k % 2][:], h[k % CH][:],
                                                ALU.mult).then_inc(zh_done, 1)
                if busy:
                    extras(q, STEPS - 1)
                if q.least == 0:
                    pool.wait_ge(in_bias, 16 * T)
                for product in q.work("conv", STEPS - 1):
                    store_ready(q, product)

            rounds(pool, body)


_INS = ["x", "adj", "nodemask", "L0_gnn_weight", "L0_gnn_w_ih", "L0_gnn_w_hh", "L0_gnn_b_ih", "L0_gnn_b_hh",
        "L1_gnn_weight", "L1_gnn_bias"]


def kernel(**inputs):
    import numpy as _np
    import concourse.bacc as _bacc
    from concourse import mybir as _mybir
    from concourse.bass_utils import run_bass_kernel_spmd as _run

    nc = _bacc.Bacc("TRN2", target_bir_lowering=False, num_devices=1)
    arrays, args = {}, []
    for name in _INS:
        a = _np.ascontiguousarray(inputs[name])
        arrays[f"in_{name}"] = a
        args.append(nc.dram_tensor(f"in_{name}", a.shape, _mybir.dt.from_np(a.dtype), kind="ExternalInput").ap())
    shape = inputs["x"].shape
    out = nc.dram_tensor("out", shape, _mybir.dt.from_np(_np.dtype("float32")), kind="ExternalOutput").ap()
    build(nc, *args, out)
    return _run(nc, [arrays], core_ids=[0]).results[0]["out"]
```
